# Optimizing a Trainium2 kernel written in Bass

```python
import numpy as np
import jax
import jax.numpy as jnp

def _softmax(x, axis=-1):
    return jax.nn.softmax(x, axis=axis)

def _gelu(x):
    return jax.nn.gelu(x, approximate=True)

def _silu(x):
    return jax.nn.silu(x)

def _sigmoid(x):
    return jax.nn.sigmoid(x)

def _layernorm(x, axis=-1, eps=1e-05):
    m = jnp.mean(x, axis=axis, keepdims=True)
    v = jnp.var(x, axis=axis, keepdims=True)
    return (x - m) / jnp.sqrt(v + eps)

def _scatter_add(tgt, idx, src, axis=0):
    return tgt.at[idx].add(src)

def _segment_sum(src, seg, n):
    return jax.ops.segment_sum(src, seg, n)
kernel_name = 'mk_flamingo_gated_d1_seqx_r4_57fc34'

def setup_inputs(seed: int=0):
    np.random.seed(seed)
    _w = jnp.asarray

    def _rec_inputs():
        import jax
        import jax.numpy as jnp
        _rk = jax.random.key(seed)
        x = 4.136e-05 + 0.9999 * jax.random.normal(jax.random.fold_in(_rk, 1), (4, 512, 256), jnp.float32)
        _lenS = 512 - jax.random.randint(jax.random.fold_in(_rk, 7), (4,), 0, max(1, 512 // 4) + 1, jnp.int32)
        _lenS2 = 512 - jax.random.randint(jax.random.fold_in(_rk, 8), (4,), 0, max(1, 512 // 4) + 1, jnp.int32)
        _ctx_2048P = jax.random.normal(jax.random.fold_in(_rk, 11), (4, 16, 512), jnp.float32)
        _ctx_2048c = jax.random.dirichlet(jax.random.fold_in(_rk, 511), 0.3 * jnp.ones((16,), jnp.float32), (4, 512))
        _ctx_2048t = jnp.einsum('bsk,bkd->bsd', _ctx_2048c, _ctx_2048P)
        _ctx_2048t = _ctx_2048t * jax.lax.rsqrt(jnp.mean(jnp.square(_ctx_2048t)) + 1e-12) * 0.953939
        ctx_2048 = -0.000392918 + 0.999932 * (_ctx_2048t + 0.3 * jax.random.normal(jax.random.fold_in(_rk, 611), (4, 512, 512), jnp.float32))
        _validS = jnp.arange(512)[None, :] < _lenS[:, None]
        _validS2 = jnp.arange(512)[None, :] < _lenS2[:, None]
        _causal = jnp.tril(jnp.ones((512, 512), dtype=bool))
        mask_BxS2_ik0 = jnp.where(jnp.broadcast_to(_validS2[:, :], (4, 512)), 0, 1).astype(jnp.int32)
        _g = jax.random.normal(jax.random.fold_in(_rk, 9001), (2, 1), jnp.float32)
        _g = jnp.sign(_g) * jnp.maximum(jnp.abs(_g), 1.0) + (_g == 0) * 1.0
        g_xattn = _g[0]
        g_ffn = _g[1]
        return (x, ctx_2048, mask_BxS2_ik0, g_xattn, g_ffn)
    x, ctx_2048, mask_BxS2_ik0, g_xattn, g_ffn = _rec_inputs()

    def _L0_xattn_setup():
        import jax, jax.numpy as jnp
        import numpy as np
        UNITS = 256
        NUM_HEADS = 8

        def _split_heads(x, n):
            B, S, D = x.shape
            return x.reshape(B, S, n, D // n).transpose(0, 2, 1, 3)
        key = jax.random.key(seed)
        k1, k2, k3 = jax.random.split(key, 3)
        B, S = (8, 256)
        memory = jax.random.normal(k1, (B, S, 2 * UNITS), dtype=jnp.float32)
        query = jax.random.normal(k2, (B, S, UNITS), dtype=jnp.float32)
        seq_mask = jax.random.randint(k3, (B, S), 0, 2, dtype=jnp.int32)
        b = jnp.zeros((1,), dtype=jnp.float32)
        return {'memory': memory, 'query': query, 'seq_mask': seq_mask, 'b': b}
    _L0_xattn_all = _L0_xattn_setup()
    _L0_xattn_in = {k: v for k, v in _L0_xattn_all.items() if k in ('b',)}
    del _L0_xattn_all

    def _L0_ffn_setup():
        import jax, jax.numpy as jnp
        import numpy as np
        DIM = 256
        HIDDEN = 768
        SCALE = 1.0 / 127.0

        def _dequant(w_int, dtype):
            return w_int.astype(dtype) * jnp.asarray(SCALE, dtype)
        key = jax.random.key(seed)
        k_x, k_g, k_u, k_d = jax.random.split(key, 4)
        x = jax.random.normal(k_x, (4, 512, DIM), dtype=jnp.float32)
        w_gate = jax.random.randint(k_g, (HIDDEN, DIM), -127, 128, dtype=jnp.int32)
        w_up = jax.random.randint(k_u, (HIDDEN, DIM), -127, 128, dtype=jnp.int32)
        w_down = jax.random.randint(k_d, (DIM, HIDDEN), -127, 128, dtype=jnp.int32)
        return {'x': x, 'w_gate': w_gate, 'w_up': w_up, 'w_down': w_down}
    _L0_ffn_all = _L0_ffn_setup()
    _L0_ffn_in = {k: v for k, v in _L0_ffn_all.items() if k in ('w_gate', 'w_up', 'w_down')}
    del _L0_ffn_all
    return {'x': x, 'ctx_2048': ctx_2048, 'mask_BxS2_ik0': mask_BxS2_ik0, 'g_xattn': g_xattn, 'g_ffn': g_ffn, 'L0_xattn_b': _L0_xattn_in['b'], 'L0_ffn_w_gate': _L0_ffn_in['w_gate'], 'L0_ffn_w_up': _L0_ffn_in['w_up'], 'L0_ffn_w_down': _L0_ffn_in['w_down']}

def reference(x, ctx_2048, mask_BxS2_ik0, g_xattn, g_ffn, L0_xattn_b, L0_ffn_w_gate, L0_ffn_w_up, L0_ffn_w_down):
    import jax
    import jax.numpy as jnp

    def _L0_xattn_ref(memory, query, seq_mask, b):
        import jax, jax.numpy as jnp
        import numpy as np
        UNITS = 256
        NUM_HEADS = 8

        def _split_heads(x, n):
            B, S, D = x.shape
            return x.reshape(B, S, n, D // n).transpose(0, 2, 1, 3)
        H = NUM_HEADS
        depth = UNITS // H
        Q = _split_heads(query, H) * depth ** (-0.5)
        k_mem, v_mem = jnp.split(memory, 2, axis=2)
        K = _split_heads(k_mem, H)
        V = _split_heads(v_mem, H)
        logits = jnp.einsum('bhqd,bhkd->bhqk', Q, K) + b[0]
        mask = seq_mask.astype(jnp.float32)[:, None, None, :]
        logits = logits + -1e+30 * (1.0 - mask)
        weights = jax.nn.softmax(logits, axis=-1)
        out = jnp.einsum('bhqk,bhkd->bhqd', weights, V)
        B, _, S, _ = out.shape
        return out.transpose(0, 2, 1, 3).reshape(B, S, UNITS)

    def _L0_ffn_ref(x, w_gate, w_up, w_down):
        import jax, jax.numpy as jnp
        import numpy as np
        DIM = 256
        HIDDEN = 768
        SCALE = 1.0 / 127.0

        def _dequant(w_int, dtype):
            return w_int.astype(dtype) * jnp.asarray(SCALE, dtype)
        wg = _dequant(w_gate, x.dtype)
        wu = _dequant(w_up, x.dtype)
        wd = _dequant(w_down, x.dtype)
        gate = jnp.einsum('bsd,hd->bsh', x, wg)
        up = jnp.einsum('bsd,hd->bsh', x, wu)
        h = jax.nn.silu(gate) * up
        return jnp.einsum('bsh,dh->bsd', h, wd)
    x = x + jnp.tanh(g_xattn[0]) * _L0_xattn_ref(ctx_2048, _layernorm(x, axis=-1), mask_BxS2_ik0, L0_xattn_b)
    x = x + jnp.tanh(g_ffn[0]) * _L0_ffn_ref(_layernorm(x, axis=-1), L0_ffn_w_gate, L0_ffn_w_up, L0_ffn_w_down)
    return x

_drawn_inputs = setup_inputs


def setup_inputs(seed=0):
    import zlib

    import numpy as np

    out = dict(_drawn_inputs(seed))
    spreads = {}
    factors = {}
    for name, (base, spread) in spreads.items():
        noise = np.random.default_rng([zlib.crc32(name.encode()), seed]).standard_normal(out[name].shape)
        drawn = base * np.exp(spread * noise) if base else spread * noise
        out[name] = jnp.asarray(drawn.astype(out[name].dtype))
    for name, factor in factors.items():
        out[name] = (out[name] * factor).astype(out[name].dtype)
    return out
```

```python
from contextlib import ExitStack

import concourse.bass as bass
from concourse import mybir

F32 = mybir.dt.float32
F16 = mybir.dt.float16
BF16 = mybir.dt.bfloat16
I32 = mybir.dt.int32
ALU = mybir.AluOpType
ACT = mybir.ActivationFunctionType
AX = mybir.AxisListType

P = 128
NH, DH = 8, 32
HG = P // DH
NG = NH // HG
NPART = 3
LN_EPS = 1e-5
MASK_STEP = -1e30
W_SCALE = 1.0 / 127.0
H_SHRINK = 1.0 / 8.0
W_LIMIT = 256.0
K_LIMIT = 60000.0


class WorkRing:

    def __init__(self, banks, emptied_by):
        self.banks, self.emptied_by, self.number, self.who, self.rank = banks, emptied_by, {}, [], []

    def copy(self):
        new = WorkRing(self.banks, self.emptied_by)
        new.number, new.who, new.rank = dict(self.number), list(self.who), list(self.rank)
        return new

    def plan(self, steps, engine_of):
        for step in steps:
            engine = engine_of(step)
            if engine is not None:
                self.number[step] = len(self.who)
                self.who.append(engine)
                self.rank.append(self.who.count(engine))
        return self

    def bank(self, step):
        return self.banks[self.number[step] % len(self.banks)]

    def filled(self, step):
        return self.number[step] + 1

    def emptied(self, step):
        n = self.number[step]
        return self.emptied_by[self.who[n]], self.rank[n]

    def before(self, step):
        n = self.number[step] - len(self.banks)
        return None if n < 0 else (self.emptied_by[self.who[n]], self.rank[n])


def emptied_by_engine(step):
    kind = step[0]
    if kind == "q_stack":
        return "act" if step[2] % 2 else "dve"
    if kind in ("mask_t", "k_stack", "flag_sum", "row_max", "attn_t", "k_block", "w_flag_sum"):
        return "dve"
    if kind in ("mask_rows", "max_t", "q_wide"):
        return "act"
    if kind == "w_t":
        return "act" if step[1] % 2 else "dve"
    return None


def attention_steps_narrow(B, QT):
    c = 3
    maxima = lambda b: [("row_max", b, c, qt, g) for qt in range(QT) for g in range(NG)]
    steps = maxima(0) + [("max_t", 0)]
    for b in range(B + 1):
        live = b < B
        ahead = maxima(b + 1) if b + 1 < B else []
        if b + 2 < B:
            steps.append(("ln", 1, b + 2))
        for slot in range(4):
            if live:
                steps.append(("scores", b, slot // 2, c, slot % 2))
            steps += ahead[3 * slot:3 * slot + 3]
            if b + 2 < B:
                steps.append(("q_stack", b + 2, slot))
            if slot == 0 and b >= 1:
                steps += [("weigh", b - 1, 1, c), ("o_copy", b - 1, 1)]
            if slot == 1 and b >= 1:
                steps.append(("attn_t", b - 1, 0))
            if slot == 2:
                if b >= 1:
                    steps.append(("attn_t", b - 1, 1))
                if live:
                    steps.append(("weigh", b, 0, c))
            if slot == 3:
                if live:
                    steps.append(("o_copy", b, 0))
                if b >= 1:
                    steps += [("attn_t", b - 1, 2), ("attn_t", b - 1, 3), ("ln", 2, b - 1)]
                if b + 1 < B:
                    steps.append(("max_t", b + 1))
        if b == 1:
            steps += [("w_check",)] + [("w_t", i) for i in range(3)]
        if b == 2:
            steps += [("w_flag_sum",)] + [("w_t", i) for i in range(3, 6)]
    return steps


def attention_steps_wide(B, QT, NC):
    steps = [("ln", 1, b) for b in range(2, B)]
    for b in range(B):
        steps += [("q_wide", b, g) for g in range(NG)]
        steps += [("k_block", b, c, g) for c in range(NC) for g in range(NG)]
        steps += [("row_max", b, c, qt, g) for c in range(NC) for qt in range(QT) for g in range(NG)]
        steps.append(("max_t", b))
        for g in range(NG):
            for c in range(NC):
                steps += [("scores", b, g, c, 0), ("scores", b, g, c, 1), ("weigh", b, g, c)]
            steps.append(("o_copy", b, g))
        steps += [("attn_t", b, qt) for qt in range(QT)] + [("ln", 2, b)]
    steps += [("w_check",), ("w_flag_sum",)] + [("w_t", i) for i in range(6)]
    return steps


def ffn_steps(B, QT, MT, wide):
    DOWN_LAG = 2
    steps = [("w_wide", i) for i in range(12)] if wide else []
    steps += [("n_t", 0, i) for i in range(QT // 2)]
    for n in range(B * MT + DOWN_LAG):
        b, m = divmod(n, MT)
        if n < B * MT:
            steps.append(("hidden", b, m))
            if m in (2, 3) and b + 1 < B:
                steps.append(("n_t", b + 1, m - 2))
        if n >= DOWN_LAG:
            d, dm = divmod(n - DOWN_LAG, MT)
            steps.append(("down", d, dm))
            if dm == MT - 1:
                steps.append(("finish", d))
    return steps


def flamingo_block_kernel(nc, x, ctx, mask, g_xattn, g_ffn, attn_b, w_gate, w_up, w_down, out):
    B, S, D = x.shape
    SK = ctx.shape[1]
    HID = w_gate.shape[0]
    QT, NC, MT, KD = S // P, SK // P, HID // P, D // P
    LAST = NC - 1
    NT = B * QT
    assert (NH * DH, ctx.shape[2], D, QT, NC) == (D, 2 * D, 256, 4, 4)
    Q_SCALE = float(DH) ** -0.5

    stack = ExitStack()
    with stack:
        def sb(name, shape, dt):
            return stack.enter_context(nc.sbuf_tensor(name, shape, dt))

        def sem(name):
            return stack.enter_context(nc.semaphore(name))

        x_sb = sb("x_sb", [P, NT, D], F32)
        kv = sb("kv", [P, B * NC, 2 * D], F32)
        norm32 = sb("norm32", [P, NT, D], F32)
        norm16 = sb("norm16", [P, 2, NT, D], F16)
        q_stacks = sb("q_stacks", [P, B, NH, S], F16)
        k_stacks = sb("k_stacks", [P, B, NH, P], F16)
        NPB = 4
        probs = sb("probs", [P, NPB, 2 * S], F32)
        o_sb = sb("o_sb", [P, 2, NG + 1, S], F32)
        w_raw = sb("w_raw", [P, 3, MT * D], I32)
        w16 = sb("w16", [P, 3, MT * D], F16)
        w_gu_t = sb("w_gu_t", [P, 2, KD, HID], F16)
        w_d_t = sb("w_d_t", [P, MT, D], F16)
        attn = sb("attn", [P, 2, D], F32)
        ident32 = sb("ident32", [P, P], F32)
        ident16 = sb("ident16", [P, P], F16)
        identb = sb("identb", [P, P], BF16)
        ones32 = sb("ones32", [P, 1], F32)
        sum_cols = sb("sum_cols", [P, NG, DH], F32)
        max_sel = sb("max_sel", [NPART * NH, NH, P], BF16)
        ones_b = sb("ones_b", [NPART, P], BF16)
        neg_half = sb("neg_half", [P, QT], F32)
        gates = sb("gates", [P, 3], F32)
        tanh_g = sb("tanh_g", [P, 2], F32)
        y_scale = sb("y_scale", [P, 1], F32)
        stats = sb("stats", [P, QT, 6], F32)
        mv = sb("mv", [P, QT, 2], F32)
        var_eps = sb("var_eps", [P, QT], F32)
        rstd = sb("rstd", [P, QT], F32)
        nbias = sb("nbias", [P, QT], F32)
        mask_raw = sb("mask_raw", [B * NC, P], I32)
        mask_f = sb("mask_f", [B * NC, P], F32)
        mask_k = sb("mask_k", [P, B * NC], F32)
        key_bias = sb("key_bias", [P, B * NC], F32)
        rest = sb("rest", [P, B * NC], F32)
        bias_parts = sb("bias_parts", [P, B * NC, NPART], BF16)
        bias_rows = sb("bias_rows", [NPART, B * NC, P], BF16)
        k_abs = sb("k_abs", [P, B], F32)
        checks = sb("checks", [P, B * NC + B], F32)
        verdict = sb("verdict", [1, 4], F32)
        attn_flag = sb("attn_flag", [1, 1], I32)
        w_abs = sb("w_abs", [P, 3], F32)
        w_over = sb("w_over", [P, 1], F32)
        w_flag = sb("w_flag", [1, 1], I32)
        max_c = sb("max_c", [P, QT, NH, NC], F32)
        neg_max = sb("neg_max", [P, QT, NH], F32)
        max_rest = sb("max_rest", [P, QT, NH], F32)
        max_parts = sb("max_parts", [P, QT, NPART, NH], BF16)
        max_rows = sb("max_rows", [NPART * NH, 2, S], BF16)
        recip = sb("recip", [P, 2, NH], F32)
        q_parts = norm16[:, :, :, :].rearrange("p l t d -> p (l t d)").rearrange(
            "p (n h a l d) -> p n h a l d", n=2 * QT, h=NH, a=2, l=2)
        k_parts = probs[:, :, :].rearrange("p n s -> p (n s)").bitcast(F16)[:, 0:B * NH * P].rearrange(
            "p (b h l a d) -> p b h l a d", b=B, h=NH, l=2, a=2)
        q_mem = q_stacks[:, :, :, :].rearrange("p b h s -> p (b h s)").bitcast(F32)
        k_blocks = q_mem[:, 0:NC * NH * P].rearrange("p (c h k) -> p c h k", c=NC, h=NH)
        q_wide = q_mem[:, NC * NH * P:NC * NH * P + NG * S].rearrange("p (g s) -> p g s", g=NG)
        n_t32 = q_mem[:, 0:KD * NT * P].rearrange("p (k s) -> p k s", k=KD)
        n_t16 = q_stacks[:, :, :, :].rearrange("p b h s -> p (b h s)")[:, 0:2 * KD * NT * P].rearrange(
            "p (l k s) -> p l k s", l=2, k=KD)
        kv_mem = kv[:, :, :].rearrange("p c d -> p (c d)")
        w_gu_t32 = kv_mem[:, 0:2 * KD * HID].rearrange("p (w k h) -> p w k h", w=2, k=KD)
        w_d_t32 = kv_mem[:, 2 * KD * HID:2 * KD * HID + MT * D].rearrange("p (m d) -> p m d", m=MT)
        w32 = kv_mem[:, 2 * KD * HID + MT * D:2 * KD * HID + MT * D + MT * D]
        probs_mem = probs[:, :, :].rearrange("p n s -> p (n s)")
        silu = probs_mem[:, 0:2 * S].rearrange("p (n s) -> p n s", n=2)
        NHB = 4
        h16 = probs_mem[:, 2 * S:2 * S + NHB * S].bitcast(F16).rearrange("p (n l s) -> p n l s", n=NHB, l=2)
        o_mem = o_sb[:, :, :, :].rearrange("p n g s -> p (n g s)")
        h32 = o_mem[:, 0:NHB * S].rearrange("p (n s) -> p n s", n=NHB)

        ps = stack.enter_context(nc.psum_tensor("ps", [P, 8, 512], F32))
        WORK, SCORES, O_BANK, D_BANK = (0, 1), 2, 6, 7

        def bank32(n):
            return ps[:, n, :]

        def bank16(n):
            return ps[:, n, :].bitcast(F16)

        def bankb(n):
            return ps[:, n, :].bitcast(BF16)

        x_loaded = [sem(f"x_loaded{b}") for b in range(B)]
        kv_loaded = [sem(f"kv_loaded{b}") for b in range(B)]
        kv_rest_loaded = sem("kv_rest_loaded")
        mask_loaded, gates_loaded = sem("mask_loaded"), sem("gates_loaded")
        w_loaded = [sem(f"w_loaded{i}") for i in range(3)]
        tanh_ready = sem("tanh_ready")
        pool_done = sem("pool_done")
        dve_done = sem("dve_done")
        mask_cast = sem("mask_cast")
        bias_split = sem("bias_split")
        checks_made = sem("checks_made")
        attn_flag_ready, w_flag_ready = sem("attn_flag_ready"), sem("w_flag_ready")
        w_checked = sem("w_checked")
        key_bias_ready = sem("key_bias_ready")
        k_high, k_low = sem("k_high"), sem("k_low")
        var_ready, rstd_ready, normed = sem("var_ready"), sem("rstd_ready"), sem("normed")
        norm_high, norm_low = sem("norm_high"), sem("norm_low")
        w_cast = sem("w_cast")
        work_filled = sem("work_filled")
        emptied_by = {"dve": sem("work_emptied_dve"), "act": sem("work_emptied_act")}
        max_split = sem("max_split")
        scores_filled, exp_done, weighed = sem("scores_filled"), sem("exp_done"), sem("weighed")
        o_copied = sem("o_copied")
        x1_ready = sem("x1_ready")
        f_filled = sem("f_filled")
        f_emptied = {"dve": sem("f_emptied_dve"), "act": sem("f_emptied_act")}
        w_wide_cast = sem("w_wide_cast")
        hid_filled, silu_done, h_made = sem("hid_filled"), sem("silu_done"), sem("h_made")
        h_high, h_low, h_used = sem("h_high"), sem("h_low"), sem("h_used")
        y_read = sem("y_read")
        stored = sem("stored")

        common = [("mask_t",), ("ln", 1, 0), ("flag_sum",), ("mask_rows", 0), ("mask_rows", 1)]
        common += [("q_stack", 0, qt) for qt in range(QT)] + [("k_stack", b) for b in range(B)]
        common += [("ln", 1, 1)] + [("q_stack", 1, qt) for qt in range(QT)]
        ring0 = WorkRing(WORK, emptied_by).plan(common, emptied_by_engine)
        narrow_steps = attention_steps_narrow(B, QT)
        wide_steps = attention_steps_wide(B, QT, NC)
        chunks_of = {False: [LAST], True: list(range(NC))}
        plans = {False: (narrow_steps, ring0.copy().plan(narrow_steps, emptied_by_engine)),
                 True: (wide_steps, ring0.copy().plan(wide_steps, emptied_by_engine))}

        def order(steps, kind):
            return {s: n for n, s in enumerate([s for s in steps if s[0] == kind])}

        ln_of = {w: order(common + plans[w][0], "ln") for w in (False, True)}

        F_WORK, Y_BANKS = (0, 1), (6, 7)

        def ffn_emptied_by(step):
            if step[0] == "n_t":
                return "act" if step[2] % 2 else "dve"
            return ("act" if step[1] % 2 else "dve") if step[0] == "w_wide" else None

        ffn_rings = {w: WorkRing(F_WORK, f_emptied).plan(ffn_steps(B, QT, MT, w), ffn_emptied_by)
                     for w in (False, True)}

        def normed_out(step, ring, wide_branch):
            _, b, i = step
            s0 = (b * QT + 2 * i) * P
            if wide_branch:
                return (n_t32[:, :, s0:s0 + 2 * P].rearrange("p k (t s) -> p k t s", t=2),
                        bank32(ring.bank(step)).rearrange("p (k t s) -> p k t s", k=KD, t=2))
            return (n_t16[:, :, :, s0:s0 + 2 * P].rearrange("p l k (t s) -> p (l k) t s", t=2),
                    bank16(ring.bank(step)).rearrange("p (k t s) -> p k t s", k=2 * KD, t=2))

        def wide_weights_out(step, ring):
            wh, part = divmod(step[1], 2)
            w, half = divmod(wh, 2)
            M2 = MT // 2
            got = bank32(ring.bank(step))[:, 0:M2 * P].rearrange("p (m k) -> p m k", m=M2)
            if w < 2:
                return (w_gu_t32[:, w, half, part * M2 * P:(part + 1) * M2 * P]
                        .rearrange("p (m k) -> p m k", m=M2), got)
            return w_d_t32[:, part * M2:(part + 1) * M2, half * P:(half + 1) * P], got

        block = stack.enter_context(nc.Block())

        def load_x(eng, b):
            eng.dma_start(x_sb[:, b * QT:(b + 1) * QT, :],
                          x[b].rearrange("(t p) d -> p t d", p=P)).then_inc(x_loaded[b], 16)

        def load_kv(eng, b):
            eng.dma_start(kv[:, b * NC + LAST, :], ctx[b, LAST * P:SK, :]).then_inc(kv_loaded[b], 16)

        @block.sync
        def _(sp):
            load_x(sp, 0)
            for b in range(0, B, 2):
                load_kv(sp, b)
            load_x(sp, 1)
            load_x(sp, 3)
            for i, w in enumerate((w_gate, w_up)):
                sp.dma_start(w_raw[:, i, :].rearrange("p (m d) -> p m d", d=D),
                             w.rearrange("(m p) d -> p m d", p=P)).then_inc(w_loaded[i], 16)
            sp.wait_ge(attn_flag_ready, 1)
            wide = sp.value_load(attn_flag[0:1, 0:1], min_val=0, max_val=1 << 20)
            with sp.If(wide > 0):
                for b in range(B):
                    sp.dma_start(kv[:, b * NC:b * NC + LAST, :],
                                 ctx[b, 0:LAST * P, :].rearrange("(c p) d -> p c d", p=P)
                                 ).then_inc(kv_rest_loaded, 16)
            for b in range(B):
                for half in range(2):
                    sp.wait_ge(y_read, 2 * b + half + 1)
                    t = b * QT + 2 * half
                    sp.dma_start(out[b, 2 * half * P:2 * (half + 1) * P, :].rearrange("(t p) d -> p t d", p=P),
                                 x_sb[:, t:t + 2, :]).then_inc(stored, 16)
            sp.wait_ge(stored, 16 * 2 * B)

        def norm_parts(step):
            _, which, b = step
            t = slice(b * QT, (b + 1) * QT)
            if which == 2:
                return norm32[:, t, :], norm16[:, 0, t, :], norm16[:, 1, t, :]
            full = norm32[:, t, :].rearrange("p t (h d) -> p (t h) d", h=NH).unsqueeze(2).to_broadcast(
                (P, QT * NH, 2, DH))
            r = slice((b % 2) * QT, (b % 2 + 1) * QT)
            return full, *(q_parts[:, r, :, :, l, :].rearrange("p t h a d -> p (t h) a d") for l in range(2))

        def key_parts(b):
            full = kv[:, b * NC + LAST, 0:D].rearrange("p (h d) -> p h d", h=NH).unsqueeze(2).to_broadcast(
                (P, NH, 2, DH))
            return full, k_parts[:, b, :, 0, :, :], k_parts[:, b, :, 1, :, :]

        def ln_pool(pool, step, place):
            pool.wait_ge(var_ready, place + 1)
            pool.tensor_tensor(rstd[:, :], var_eps[:, :], neg_half[:, :], ALU.pow).then_inc(rstd_ready, 1)
            pool.wait_ge(norm_high, place + 1)
            full, high, low = norm_parts(step)
            pool.tensor_tensor(low, full, high, ALU.subtract).then_inc(norm_low, 1)

        @block.gpsimd
        def _(pool):
            pool.memset(neg_half[:, :], -0.5).then_inc(pool_done, 1)
            pool.memset(ident32[:, :], 0.0).then_inc(pool_done, 1)
            pool.memset(ident16[:, :], 0.0).then_inc(pool_done, 1)
            pool.memset(identb[:, :], 0.0).then_inc(pool_done, 1)
            pool.memset(sum_cols[:, :, :], 0.0).then_inc(pool_done, 1)
            pool.memset(max_sel[:, :, :], 0.0).then_inc(pool_done, 1)
            pool.memset(ones_b[:, :], 1.0).then_inc(pool_done, 1)
            pool.memset(ones32[:, :], 1.0).then_inc(pool_done, 1)
            pool.wait_ge(pool_done, 8)
            for n, m in enumerate((ident32, ident16, identb)):
                pool.affine_select(out=m[:, :], in_=m[:, :], compare_op=ALU.not_equal, fill=1.0, base=0,
                                   pattern=[[-1, P]], channel_multiplier=1).then_inc(pool_done, 1)
            pool.affine_select(out=sum_cols[:, :, :], in_=sum_cols[:, :, :], compare_op=ALU.not_equal, fill=1.0,
                               base=0, pattern=[[-1, NG], [1, DH]], channel_multiplier=0).then_inc(pool_done, 1)
            for part in range(NPART):
                pool.affine_select(out=max_sel[:, :, :], in_=max_sel[:, :, :], compare_op=ALU.not_equal,
                                   fill=1.0, base=-NH * part, pattern=[[-1, NH], [0, P]],
                                   channel_multiplier=1).then_inc(pool_done, 1)
                pool.wait_ge(pool_done, 13 + part)

            def common_pool():
                for step in common:
                    if step[0] == "ln":
                        ln_pool(pool, step, ln_of[False][step])
                    if step == ("ln", 1, 0):
                        for b in range(B):
                            pool.wait_ge(k_high, b + 1)
                            full, high, low = key_parts(b)
                            pool.tensor_tensor(low, full, high, ALU.subtract).then_inc(k_low, 1)

            common_pool()
            for i in range(3):
                pool.wait_ge(w_loaded[i], 16)
                pool.tensor_copy(w16[:, i, :], w_raw[:, i, :]).then_inc(w_cast, 1)

            def attention_pool(wide_branch):
                steps, ring = plans[wide_branch]
                place = order(steps, "attn_t")
                for step in steps:
                    if step[0] == "ln":
                        ln_pool(pool, step, ln_of[wide_branch][step])
                    elif step[0] == "attn_t":
                        n = place[step]
                        t = step[1] * QT + step[2]
                        pool.wait_ge(*ring.emptied(step))
                        pool.tensor_tensor(x_sb[:, t, :], x_sb[:, t, :], attn[:, n % 2, :],
                                           ALU.add).then_inc(x1_ready, 1)

            pool.wait_ge(attn_flag_ready, 1)
            wide = pool.value_load(attn_flag[0:1, 0:1], min_val=0, max_val=1 << 20)
            with pool.If(wide > 0):
                attention_pool(True)
            with pool.Else():
                attention_pool(False)

        def ln_act(act, step, place):
            _, which, b = step
            act.wait_ge(normed, place + 1)
            if which == 1 and b >= 2:
                act.wait_ge(work_filled, (ring0 if b - 2 < 2 else plans[False][1]).filled(("q_stack", b - 2, QT - 1)))
            full, high, _ = norm_parts(step)
            act.activation(high, full, ACT.Copy).then_inc(norm_high, 1)

        def q_stack_out(step, ring):
            _, b, qt = step
            return (q_stacks[:, b, :, qt * P:(qt + 1) * P],
                    bank16(ring.bank(step)).rearrange("p (h k) -> p h k", h=NH))

        def weights_out(step, ring):
            w, half = divmod(step[1], 2)
            got = bank16(ring.bank(step))[:, 0:MT * P].rearrange("p (m k) -> p m k", m=MT)
            if w < 2:
                return w_gu_t[:, w, half, :].rearrange("p (m k) -> p m k", m=MT), got
            return w_d_t[:, :, half * P:(half + 1) * P], got

        @block.scalar
        def _(act):
            act.dma_start(mask_raw[:, :], mask.rearrange("b (c k) -> (b c) k", k=P)).then_inc(mask_loaded, 16)
            for n, g in enumerate((g_xattn, g_ffn, attn_b)):
                act.dma_start(gates[:, n:n + 1], g.partition_broadcast(P)).then_inc(gates_loaded, 16)
            for b in range(1, B, 2):
                load_kv(act, b)
            load_x(act, 2)
            act.dma_start(w_raw[:, 2, :].rearrange("p (t h) -> p t h", h=HID),
                          w_down.rearrange("(t p) h -> p t h", p=P)).then_inc(w_loaded[2], 16)
            act.wait_ge(gates_loaded, 48)
            act.activation(tanh_g[:, :], gates[:, 0:2], ACT.Tanh).then_inc(tanh_ready, 1)

            def mask_rows_copy(step, ring):
                half = step[1]
                act.wait_ge(work_filled, ring.filled(step))
                per = B * NC // 2
                act.activation(bias_rows[:, half * per:(half + 1) * per, :],
                               bankb(ring.bank(step))[0:NPART, :].rearrange("p (c k) -> p c k", k=P),
                               ACT.Copy).then_inc(emptied_by["act"], 1)

            for step in common:
                if step[0] == "ln":
                    ln_act(act, step, ln_of[False][step])
                if step == ("ln", 1, 0):
                    for b in range(B):
                        act.wait_ge(kv_loaded[b], 16)
                        full, high, _ = key_parts(b)
                        act.activation(high, full, ACT.Copy).then_inc(k_high, 1)
                if step[0] == "mask_rows":
                    mask_rows_copy(step, ring0)
                if step[0] == "q_stack" and emptied_by_engine(step) == "act":
                    act.wait_ge(work_filled, ring0.filled(step))
                    act.activation(*q_stack_out(step, ring0), ACT.Copy).then_inc(emptied_by["act"], 1)

            def attention_act(wide_branch):
                steps, ring = plans[wide_branch]
                pair_of, unit_of = order(steps, "scores"), order(steps, "weigh")
                act.wait_ge(key_bias_ready, 1)
                for step in steps:
                    kind = step[0]
                    if kind == "ln":
                        ln_act(act, step, ln_of[wide_branch][step])
                    elif kind in ("q_stack", "w_t") and emptied_by_engine(step) == "act":
                        act.wait_ge(work_filled, ring.filled(step))
                        dst, src = q_stack_out(step, ring) if kind == "q_stack" else weights_out(step, ring)
                        act.activation(dst, src, ACT.Copy).then_inc(emptied_by["act"], 1)
                    elif kind == "q_wide":
                        act.wait_ge(work_filled, ring.filled(step))
                        act.activation(q_wide[:, step[2], :], bank32(ring.bank(step)),
                                       ACT.Copy).then_inc(emptied_by["act"], 1)
                    elif kind == "max_t":
                        act.wait_ge(work_filled, ring.filled(step))
                        act.activation(max_rows[:, step[1] % 2, :], bankb(ring.bank(step))[0:NPART * NH, 0:S],
                                       ACT.Copy).then_inc(emptied_by["act"], 1)
                    elif kind == "scores":
                        _, b, g, c, _ = step
                        j = pair_of[step]
                        act.wait_ge(scores_filled, j + 1)
                        if j >= NPB:
                            act.wait_ge(weighed, (j - NPB) // 2 + 1)
                        n = b * NC + c
                        act.activation(probs[:, j % NPB, :],
                                       ps[:, SCORES + 2 * (j % 2):SCORES + 2 * (j % 2) + 2, :], ACT.Exp,
                                       bias=key_bias[:, n:n + 1]).then_inc(exp_done, 1)
                    elif kind == "o_copy":
                        _, b, g = step
                        act.wait_ge(weighed, unit_of[("weigh", b, g, chunks_of[wide_branch][-1])] + 1)
                        if b >= 2 and g == 0:
                            act.wait_ge(work_filled, ring.filled(("attn_t", b - 2, QT - 1)))
                        act.activation(o_sb[:, b % 2, g, :], bank32(O_BANK), ACT.Copy).then_inc(o_copied, 1)
                        if g == NG - 1:
                            act.activation(o_sb[:, b % 2, NG, :], bank32(D_BANK), ACT.Copy).then_inc(o_copied, 1)

            act.wait_ge(attn_flag_ready, 1)
            wide = act.value_load(attn_flag[0:1, 0:1], min_val=0, max_val=1 << 20)
            with act.If(wide > 0):
                attention_act(True)
            with act.Else():
                attention_act(False)

            def ffn_act(wide_branch):
                steps = ffn_steps(B, QT, MT, wide_branch)
                ring = ffn_rings[wide_branch]
                for step in steps:
                    kind = step[0]
                    if kind in ("n_t", "w_wide") and ffn_emptied_by(step) == "act":
                        act.wait_ge(f_filled, ring.filled(step))
                        if kind == "n_t":
                            dst, src = normed_out(step, ring, wide_branch)
                        else:
                            dst, src = wide_weights_out(step, ring)
                        act.activation(dst, src, ACT.Copy).then_inc(f_emptied["act"], 1)
                    elif kind == "hidden":
                        n = step[1] * MT + step[2]
                        act.wait_ge(hid_filled, n + 1)
                        if n >= 2:
                            act.wait_ge(h_made, n - 1)
                        act.activation(silu[:, n % 2, :], bank32(SCORES + 2 * (n % 2)), ACT.Silu,
                                       scale=W_SCALE).then_inc(silu_done, 1)
                        if n >= 1 and not wide_branch:
                            high_part(n - 1)
                if not wide_branch:
                    high_part(B * MT - 1)

            def high_part(n):
                act.wait_ge(h_made, n + 1)
                if n >= NHB:
                    act.wait_ge(h_used, n - NHB + 1)
                act.activation(h16[:, n % NHB, 0, :], h32[:, n % NHB, :], ACT.Copy).then_inc(h_high, 1)

            act.wait_ge(w_flag_ready, 1)
            wide_w = act.value_load(w_flag[0:1, 0:1], min_val=0, max_val=1 << 20)
            with act.If(wide_w > 0):
                ffn_act(True)
            with act.Else():
                ffn_act(False)

        @block.vector
        def _(dve):
            count = [0]

            def mine(ins):
                ins.then_inc(dve_done, 1)
                count[0] += 1

            def wait_mine():
                dve.wait_ge(dve_done, count[0])

            def ln_dve(step, place):
                _, which, b = step
                t0 = b * QT
                if which == 1:
                    dve.wait_ge(x_loaded[b], 16)
                else:
                    dve.wait_ge(x1_ready, QT * (b + 1))
                    dve.wait_ge(norm_low, b + 1)
                    dve.wait_ge(norm_high, b + 1)
                for i in range(QT):
                    mine(dve.bn_stats(stats[:, i, :], x_sb[:, t0 + i, :]))
                wait_mine()
                for i in range(QT):
                    mine(dve.bn_aggr(mv[:, i, :], stats[:, i, :]))
                wait_mine()
                if place >= 1:
                    dve.wait_ge(rstd_ready, place)
                dve.tensor_scalar(var_eps[:, :], mv[:, :, 1], LN_EPS, None, ALU.add).then_inc(var_ready, 1)
                dve.wait_ge(rstd_ready, place + 1)
                if which == 1:
                    mine(dve.tensor_scalar(rstd[:, :], rstd[:, :], Q_SCALE, None, ALU.mult))
                    wait_mine()
                mine(dve.scalar_tensor_tensor(out=nbias[:, :], in0=mv[:, :, 0], scalar=-1.0, in1=rstd[:, :],
                                              op0=ALU.mult, op1=ALU.mult))
                wait_mine()
                for i in range(QT):
                    ins = dve.tensor_scalar(norm32[:, t0 + i, :], x_sb[:, t0 + i, :], rstd[:, i:i + 1],
                                            nbias[:, i:i + 1], ALU.mult, ALU.add)
                ins.then_inc(normed, 1)

            def mask_steps():
                dve.wait_ge(mask_loaded, 16)
                dve.tensor_copy(mask_f[:, :], mask_raw[:, :]).then_inc(mask_cast, 1)
                step = ("mask_t",)
                dve.wait_ge(work_filled, ring0.filled(step))
                dve.tensor_copy(mask_k[:, :], bank32(ring0.bank(step))[:, 0:B * NC]).then_inc(emptied_by["dve"], 1)
                dve.wait_ge(*ring0.emptied(step))
                mine(dve.tensor_scalar(key_bias[:, :], mask_k[:, :], -1.0, 1.0, ALU.mult, ALU.add))
                mine(dve.tensor_scalar(checks[:, 0:B * NC], mask_k[:, :], 0.0, None, ALU.not_equal))
                last = mask_k[:, :].rearrange("p (b c) -> p b c", c=NC)[:, :, LAST]
                mine(dve.tensor_scalar(checks[:, B * NC:B * NC + B], last, 1.0, None, ALU.is_ge))
                wait_mine()
                dve.wait_ge(gates_loaded, 48)
                mine(dve.tensor_scalar(key_bias[:, :], key_bias[:, :], MASK_STEP, gates[:, 2:3], ALU.mult, ALU.add))
                wait_mine()
                dve.tensor_scalar(key_bias[:, :], key_bias[:, :], 3e38, -3e38, ALU.min, ALU.max
                                  ).then_inc(key_bias_ready, 1)
                dve.wait_ge(key_bias_ready, 1)
                mine(dve.tensor_copy(bias_parts[:, :, 0], key_bias[:, :]))
                wait_mine()
                mine(dve.tensor_tensor(rest[:, :], key_bias[:, :], bias_parts[:, :, 0], ALU.subtract))
                wait_mine()
                mine(dve.tensor_copy(bias_parts[:, :, 1], rest[:, :]))
                wait_mine()
                dve.tensor_tensor(bias_parts[:, :, 2], rest[:, :], bias_parts[:, :, 1], ALU.subtract
                                  ).then_inc(bias_split, 1)

            def key_checks():
                for b in range(B):
                    dve.wait_ge(kv_loaded[b], 16)
                    mine(dve.tensor_reduce(k_abs[:, b:b + 1], kv[:, b * NC + LAST, 0:D], AX.X, ALU.max,
                                           apply_absolute_value=True))
                wait_mine()
                slot = checks[:, 0:B * NC].rearrange("p (b c) -> p b c", c=NC)[:, :, LAST]
                dve.tensor_scalar(slot, k_abs[:, :], K_LIMIT, None, ALU.is_gt).then_inc(checks_made, 1)

            def attn_verdict():
                step = ("flag_sum",)
                dve.wait_ge(work_filled, ring0.filled(step))
                counts = bank32(ring0.bank(step))
                mine(dve.tensor_reduce(verdict[:, 0:1], counts[0:1, 0:B * NC], AX.X, ALU.add))
                dve.tensor_reduce(verdict[:, 1:2], counts[0:1, B * NC:B * NC + B], AX.X, ALU.min
                                  ).then_inc(emptied_by["dve"], 1)
                wait_mine()
                dve.wait_ge(*ring0.emptied(step))
                dve.scalar_tensor_tensor(out=attn_flag[:, :], in0=verdict[:, 1:2], scalar=1.0,
                                         in1=verdict[:, 0:1], op0=ALU.is_lt, op1=ALU.add
                                         ).then_inc(attn_flag_ready, 1)

            mask_steps()
            for step in common:
                if step[0] == "ln":
                    ln_dve(step, ln_of[False][step])
                    if step == ("ln", 1, 0):
                        key_checks()
                elif step[0] == "flag_sum":
                    attn_verdict()
                elif step[0] == "q_stack" and emptied_by_engine(step) == "dve":
                    dve.wait_ge(work_filled, ring0.filled(step))
                    dve.tensor_copy(*q_stack_out(step, ring0)).then_inc(emptied_by["dve"], 1)
                elif step[0] == "k_stack":
                    dve.wait_ge(work_filled, ring0.filled(step))
                    dve.tensor_copy(k_stacks[:, step[1], :, :],
                                    bank16(ring0.bank(step)).rearrange("p (h k) -> p h k", h=NH)
                                    ).then_inc(emptied_by["dve"], 1)
            dve.wait_ge(tanh_ready, 1)
            mine(dve.tensor_scalar(y_scale[:, :], tanh_g[:, 1:2], W_SCALE / H_SHRINK, None, ALU.mult))
            wait_mine()

            def attention_dve(wide_branch):
                steps, ring = plans[wide_branch]
                chunks = chunks_of[wide_branch]
                attn_of = order(steps, "attn_t")
                if wide_branch:
                    for b in range(2):
                        for qt in range(QT):
                            dve.wait_ge(*ring.emptied(("q_stack", b, qt)))
                    mine(dve.memset(k_blocks, 0.0))
                    wait_mine()
                for step in steps:
                    kind = step[0]
                    if kind == "ln":
                        ln_dve(step, ln_of[wide_branch][step])
                    elif kind in ("q_stack", "w_t") and emptied_by_engine(step) == "dve":
                        dve.wait_ge(work_filled, ring.filled(step))
                        dst, src = q_stack_out(step, ring) if kind == "q_stack" else weights_out(step, ring)
                        dve.tensor_copy(dst, src).then_inc(emptied_by["dve"], 1)
                    elif kind == "k_block":
                        _, b, c, g = step
                        dve.wait_ge(work_filled, ring.filled(step))
                        for j in range(HG):
                            rows = slice(j * DH, (j + 1) * DH)
                            ins = dve.tensor_copy(k_blocks[rows, c, g * HG + j, :],
                                                  bank32(ring.bank(step))[rows, 0:P])
                        ins.then_inc(emptied_by["dve"], 1)
                    elif kind == "row_max":
                        _, b, c, qt, g = step
                        dve.wait_ge(work_filled, ring.filled(step))
                        if qt == 0 and g == 0 and c == chunks[0] and b >= 1:
                            dve.wait_ge(max_split, b)
                        one = len(chunks) == 1
                        dst = neg_max[:, qt, g * HG:(g + 1) * HG] if one else max_c[:, qt, g * HG:(g + 1) * HG, c]
                        dve.tensor_reduce(dst, bank32(ring.bank(step)).rearrange("p (h k) -> p h k", h=HG),
                                          AX.X, ALU.max, negate=one).then_inc(emptied_by["dve"], 1)
                    elif kind == "max_t":
                        b = step[1]
                        dve.wait_ge(*ring.emptied(("row_max", b, chunks[-1], QT - 1, NG - 1)))
                        if b >= 1:
                            dve.wait_ge(work_filled, ring.filled(("max_t", b - 1)))
                        if len(chunks) > 1:
                            mine(dve.tensor_reduce(neg_max[:, :, :], max_c[:, :, :, :], AX.X, ALU.max, negate=True))
                            wait_mine()
                        mine(dve.tensor_copy(max_parts[:, :, 0, :], neg_max[:, :, :]))
                        wait_mine()
                        mine(dve.tensor_tensor(max_rest[:, :, :], neg_max[:, :, :], max_parts[:, :, 0, :],
                                               ALU.subtract))
                        wait_mine()
                        mine(dve.tensor_copy(max_parts[:, :, 1, :], max_rest[:, :, :]))
                        wait_mine()
                        dve.tensor_tensor(max_parts[:, :, 2, :], max_rest[:, :, :], max_parts[:, :, 1, :],
                                          ALU.subtract).then_inc(max_split, 1)
                    elif kind == "attn_t":
                        _, b, qt = step
                        n = attn_of[step]
                        got = bank32(ring.bank(step))
                        dve.wait_ge(work_filled, ring.filled(step))
                        if n >= 2:
                            dve.wait_ge(x1_ready, n - 1)
                        sums = got[:, NG * P:(NG + 1) * P].rearrange("p (j d) -> p d j", d=DH)[:, 0:NG, :]
                        mine(dve.reciprocal(recip[:, n % 2, :].rearrange("p (g j) -> p g j", g=NG), sums))
                        wait_mine()
                        dve.scalar_tensor_tensor(
                            out=attn[:, n % 2, :].rearrange("p (h d) -> p h d", d=DH),
                            in0=got[:, 0:NG * P].rearrange("p (h d) -> p h d", d=DH), scalar=tanh_g[:, 0:1],
                            in1=recip[:, n % 2, :].unsqueeze(2).to_broadcast((P, NH, DH)),
                            op0=ALU.mult, op1=ALU.mult).then_inc(emptied_by["dve"], 1)
                    elif kind == "w_check":
                        for i in range(3):
                            dve.wait_ge(w_loaded[i], 16)
                            mine(dve.tensor_reduce(w_abs[:, i:i + 1], w_raw[:, i, :], AX.X, ALU.max,
                                                   apply_absolute_value=True))
                        wait_mine()
                        mine(dve.tensor_reduce(w_over[:, :], w_abs[:, :], AX.X, ALU.max))
                        wait_mine()
                        dve.tensor_scalar(w_over[:, :], w_over[:, :], W_LIMIT, None, ALU.is_gt).then_inc(w_checked, 1)
                    elif kind == "w_flag_sum":
                        dve.wait_ge(work_filled, ring.filled(step))
                        dve.tensor_copy(verdict[:, 2:3], bank32(ring.bank(step))[0:1, 0:1]
                                        ).then_inc(emptied_by["dve"], 1)
                        dve.wait_ge(*ring.emptied(step))
                        dve.tensor_copy(w_flag[:, :], verdict[:, 2:3]).then_inc(w_flag_ready, 1)

            dve.wait_ge(attn_flag_ready, 1)
            wide = dve.value_load(attn_flag[0:1, 0:1], min_val=0, max_val=1 << 20)
            at_branch = count[0]
            with dve.If(wide > 0):
                attention_dve(True)
            count[0] = at_branch
            with dve.Else():
                attention_dve(False)

            def ffn_dve(wide_branch):
                ring = ffn_rings[wide_branch]
                steps = ffn_steps(B, QT, MT, wide_branch)
                for step in steps:
                    kind = step[0]
                    if kind == "w_wide" and step[1] % 4 == 0:
                        if step[1]:
                            dve.wait_ge(f_filled, ring.filled(("w_wide", step[1] - 1)))
                        dve.tensor_copy(w32, w_raw[:, step[1] // 4, :]).then_inc(w_wide_cast, 1)
                    if kind in ("n_t", "w_wide") and ffn_emptied_by(step) == "dve":
                        dve.wait_ge(f_filled, ring.filled(step))
                        if kind == "n_t":
                            dst, src = normed_out(step, ring, wide_branch)
                        else:
                            dst, src = wide_weights_out(step, ring)
                        dve.tensor_copy(dst, src).then_inc(f_emptied["dve"], 1)
                    elif kind == "hidden":
                        n = step[1] * MT + step[2]
                        dve.wait_ge(silu_done, n + 1)
                        if n >= NHB:
                            dve.wait_ge(h_used, n - NHB + 1)
                        dve.scalar_tensor_tensor(out=h32[:, n % NHB, :], in0=bank32(SCORES + 2 * (n % 2) + 1),
                                                 scalar=W_SCALE * H_SHRINK, in1=silu[:, n % 2, :],
                                                 op0=ALU.mult, op1=ALU.mult).then_inc(h_made, 1)
                        if n >= 1 and not wide_branch:
                            low_part(n - 1)
                        if n == B * MT - 1 and not wide_branch:
                            low_part(n)
                    elif kind == "finish":
                        b = step[1]
                        for half in range(2):
                            for i in range(2):
                                t = b * QT + 2 * half + i
                                dve.wait_ge(h_used, MT * (b + 1))
                                ins = dve.scalar_tensor_tensor(
                                    out=x_sb[:, t, :], in0=ps[:, Y_BANKS[half], i * D:(i + 1) * D],
                                    scalar=y_scale[:, 0:1], in1=x_sb[:, t, :], op0=ALU.mult, op1=ALU.add)
                            ins.then_inc(y_read, 1)

            def low_part(n):
                dve.wait_ge(h_high, n + 1)
                dve.tensor_tensor(h16[:, n % NHB, 1, :], h32[:, n % NHB, :], h16[:, n % NHB, 0, :],
                                  ALU.subtract).then_inc(h_low, 1)

            dve.wait_ge(w_flag_ready, 1)
            wide_w = dve.value_load(w_flag[0:1, 0:1], min_val=0, max_val=1 << 20)
            with dve.If(wide_w > 0):
                ffn_dve(True)
            with dve.Else():
                ffn_dve(False)

        @block.tensor
        def _(pe):
            pe.wait_ge(pool_done, 12 + NPART)

            def open_work(step, ring):
                last = ring.before(step)
                if last is not None:
                    pe.wait_ge(*last)
                return ring.bank(step)

            def stack_q(step, ring, place):
                _, b, qt = step
                n = open_work(step, ring)
                pe.wait_ge(norm_high, place + 1)
                pe.wait_ge(norm_low, place + 1)
                for h in range(NH):
                    src = q_parts[:, (b % 2) * QT + qt, h, :, :, :].rearrange("p a l d -> p (a l d)")
                    ins = pe.transpose(bank16(n)[:, h * P:(h + 1) * P], src, ident16[:, :])
                ins.then_inc(work_filled, 1)

            for step in common:
                kind = step[0]
                if kind == "mask_t":
                    n = open_work(step, ring0)
                    pe.wait_ge(mask_cast, 1)
                    pe.transpose(bank32(n)[:, 0:B * NC], mask_f[:, :], ident32[0:B * NC, 0:B * NC]
                                 ).then_inc(work_filled, 1)
                elif kind == "flag_sum":
                    n = open_work(step, ring0)
                    pe.wait_ge(checks_made, 1)
                    pe.matmul(bank32(n)[0:1, 0:B * NC + B], ones32[:, 0:1], checks[:, :], start=True, stop=True
                              ).then_inc(work_filled, 1)
                elif kind == "mask_rows":
                    n = open_work(step, ring0)
                    pe.wait_ge(bias_split, 1)
                    per = B * NC // 2
                    for i in range(per):
                        ins = pe.transpose(bankb(n)[0:NPART, i * P:(i + 1) * P],
                                           bias_parts[:, step[1] * per + i, :], identb[:, :])
                    ins.then_inc(work_filled, 1)
                elif kind == "q_stack":
                    stack_q(step, ring0, step[1])
                elif kind == "k_stack":
                    b = step[1]
                    n = open_work(step, ring0)
                    pe.wait_ge(k_high, b + 1)
                    pe.wait_ge(k_low, b + 1)
                    for h in range(NH):
                        src = k_parts[:, b, h, :, :, :].rearrange("p l a d -> p (l a d)")
                        ins = pe.transpose(bank16(n)[:, h * P:(h + 1) * P], src, ident16[:, :])
                    ins.then_inc(work_filled, 1)

            def attention_pe(wide_branch):
                steps, ring = plans[wide_branch]
                chunks = chunks_of[wide_branch]
                pair_of, unit_of = order(steps, "scores"), order(steps, "weigh")
                pe.wait_ge(*ring.emptied(("mask_rows", 1)))
                for step in steps:
                    kind = step[0]
                    if kind == "q_stack":
                        stack_q(step, ring, ln_of[wide_branch][("ln", 1, step[1])])
                    elif kind == "q_wide":
                        _, b, g = step
                        n = open_work(step, ring)
                        pe.wait_ge(normed, ln_of[wide_branch][("ln", 1, b)] + 1)
                        for qt in range(QT):
                            ins = pe.transpose(bank32(n)[:, qt * P:(qt + 1) * P],
                                               norm32[:, b * QT + qt, g * P:(g + 1) * P], ident32[:, :])
                        ins.then_inc(work_filled, 1)
                    elif kind == "k_block":
                        _, b, c, g = step
                        n = open_work(step, ring)
                        pe.wait_ge(kv_rest_loaded, 16 * B)
                        pe.wait_ge(kv_loaded[b], 16)
                        pe.transpose(bank32(n)[:, 0:P], kv[:, b * NC + c, g * P:(g + 1) * P], ident32[:, :]
                                     ).then_inc(work_filled, 1)
                    elif kind == "row_max":
                        _, b, c, qt, g = step
                        n = open_work(step, ring)
                        if wide_branch:
                            pe.wait_ge(*ring.emptied(("q_wide", b, g)))
                            pe.wait_ge(*ring.emptied(("k_block", b, c, g)))
                            pe.matmul(bank32(n), q_wide[:, g, qt * P:(qt + 1) * P],
                                      k_blocks[:, c, g * HG:(g + 1) * HG, :], start=True, stop=False)
                        else:
                            pe.wait_ge(*ring.emptied(("q_stack", b, qt)))
                            pe.wait_ge(*ring.emptied(("k_stack", b)))
                            for j in range(HG):
                                h = g * HG + j
                                pe.matmul(bank32(n)[:, j * P:(j + 1) * P], q_stacks[:, b, h, qt * P:(qt + 1) * P],
                                          k_stacks[:, b, h, :], start=(j == 0), stop=False, skip_group_check=True)
                        rows = bias_rows[:, b * NC + c, :].unsqueeze(1).to_broadcast((NPART, HG, P))
                        pe.matmul(bank32(n), ones_b[:, :], rows, start=False, stop=True, skip_group_check=True
                                  ).then_inc(work_filled, 1)
                    elif kind == "max_t":
                        n = open_work(step, ring)
                        pe.wait_ge(max_split, step[1] + 1)
                        for qt in range(QT):
                            ins = pe.transpose(bankb(n)[0:NPART * NH, qt * P:(qt + 1) * P],
                                               max_parts[:, qt, :, :].rearrange("p a h -> p (a h)"), identb[:, :])
                        ins.then_inc(work_filled, 1)
                    elif kind == "scores":
                        _, b, g, c, pair = step
                        j = pair_of[step]
                        if j >= 2:
                            pe.wait_ge(exp_done, j - 1)
                        pe.wait_ge(*ring.emptied(("max_t", b)))
                        if not wide_branch and pair == 0 and g == 0:
                            for qt in range(QT):
                                pe.wait_ge(*ring.emptied(("q_stack", b, qt)))
                        for i in range(2):
                            h = g * HG + 2 * pair + i
                            dst = bank32(SCORES + 2 * (j % 2) + i)
                            if wide_branch:
                                pe.matmul(dst, k_blocks[:, c, h, :], q_wide[:, g, :], start=True, stop=False)
                            else:
                                pe.matmul(dst, k_stacks[:, b, h, :], q_stacks[:, b, h, :], start=True, stop=False)
                            ins = pe.matmul(dst, max_sel[:, h, :], max_rows[:, b % 2, :], start=False, stop=True)
                        ins.then_inc(scores_filled, 1)
                    elif kind == "weigh":
                        _, b, g, c = step
                        u = unit_of[step]
                        first, last = c == chunks[0], c == chunks[-1]
                        pe.wait_ge(exp_done, 2 * u + 2)
                        copies = b * (NG + 1)
                        if first and copies + g > 0:
                            pe.wait_ge(o_copied, copies + g)
                        for j in range(HG):
                            h = g * HG + j
                            part = slice(j * DH, (j + 1) * DH)
                            pr = probs[:, (2 * u + j // 2) % NPB, (j % 2) * S:(j % 2 + 1) * S]
                            pe.matmul(ps[part, O_BANK, :], kv[:, b * NC + c, D + h * DH:D + (h + 1) * DH], pr,
                                      start=first, stop=last, tile_position=(0, j * DH))
                        for j in range(HG):
                            part = slice(j * DH, (j + 1) * DH)
                            pr = probs[:, (2 * u + j // 2) % NPB, (j % 2) * S:(j % 2 + 1) * S]
                            ins = pe.matmul(ps[part, D_BANK, :], sum_cols[:, g, :], pr,
                                            start=(first and g == 0), stop=(last and g == NG - 1),
                                            tile_position=(0, j * DH))
                        ins.then_inc(weighed, 1)
                    elif kind == "attn_t":
                        _, b, qt = step
                        n = open_work(step, ring)
                        pe.wait_ge(o_copied, (b + 1) * (NG + 1))
                        for g in range(NG + 1):
                            ins = pe.transpose(bank32(n)[:, g * P:(g + 1) * P],
                                               o_sb[:, b % 2, g, qt * P:(qt + 1) * P], ident32[:, :])
                        ins.then_inc(work_filled, 1)
                    elif kind == "w_flag_sum":
                        n = open_work(step, ring)
                        pe.wait_ge(w_checked, 1)
                        pe.matmul(bank32(n)[0:1, 0:1], ones32[:, 0:1], w_over[:, :], start=True, stop=True
                                  ).then_inc(work_filled, 1)
                    elif kind == "w_t":
                        w, half = divmod(step[1], 2)
                        n = open_work(step, ring)
                        pe.wait_ge(w_cast, w + 1)
                        for m in range(MT):
                            at = m * D + half * P if w < 2 else half * HID + m * P
                            ins = pe.transpose(bank16(n)[:, m * P:(m + 1) * P], w16[:, w, at:at + P], ident16[:, :])
                        ins.then_inc(work_filled, 1)

                pe.wait_ge(exp_done, len(pair_of))
                pe.wait_ge(o_copied, B * (NG + 1))
                for engine in emptied_by:
                    pe.wait_ge(emptied_by[engine], ring.who.count(engine))

            pe.wait_ge(attn_flag_ready, 1)
            wide = pe.value_load(attn_flag[0:1, 0:1], min_val=0, max_val=1 << 20)
            with pe.If(wide > 0):
                attention_pe(True)
            with pe.Else():
                attention_pe(False)

            def ffn_pe(wide_branch):
                ring = ffn_rings[wide_branch]
                steps = ffn_steps(B, QT, MT, wide_branch)
                for step in steps:
                    kind = step[0]
                    if kind == "w_wide":
                        wh, part = divmod(step[1], 2)
                        w, half = divmod(wh, 2)
                        n = open_work(step, ring)
                        pe.wait_ge(w_wide_cast, w + 1)
                        for i in range(MT // 2):
                            m = part * (MT // 2) + i
                            at = m * D + half * P if w < 2 else half * HID + m * P
                            ins = pe.transpose(bank32(n)[:, i * P:(i + 1) * P], w32[:, at:at + P], ident32[:, :])
                        ins.then_inc(f_filled, 1)
                    elif kind == "n_t":
                        _, b, i = step
                        n = open_work(step, ring)
                        place = B + b + 1
                        pe.wait_ge(normed, place)
                        pe.wait_ge(norm_high, place)
                        pe.wait_ge(norm_low, place)
                        for lk in range(KD if wide_branch else 2 * KD):
                            for t in range(2):
                                tile = b * QT + 2 * i + t
                                at = slice((2 * lk + t) * P, (2 * lk + t + 1) * P)
                                l, k = divmod(lk, KD)
                                if wide_branch:
                                    ins = pe.transpose(bank32(n)[:, at], norm32[:, tile, k * P:(k + 1) * P],
                                                       ident32[:, :])
                                else:
                                    ins = pe.transpose(bank16(n)[:, at], norm16[:, l, tile, k * P:(k + 1) * P],
                                                       ident16[:, :])
                        ins.then_inc(f_filled, 1)
                    elif kind == "hidden":
                        _, b, m = step
                        n = b * MT + m
                        if m == 0:
                            for i in range(QT // 2):
                                pe.wait_ge(*ring.emptied(("n_t", b, i)))
                            if n == 0 and wide_branch:
                                for i in range(12):
                                    pe.wait_ge(*ring.emptied(("w_wide", i)))
                        if n >= 2:
                            pe.wait_ge(h_made, n - 1)
                        for w in range(2):
                            dst = bank32(SCORES + 2 * (n % 2) + w)
                            terms = [(k, l) for k in range(KD) for l in range(1 if wide_branch else 2)]
                            for k, l in terms:
                                at = slice(m * P, (m + 1) * P)
                                if wide_branch:
                                    lhs, rhs = w_gu_t32[:, w, k, at], n_t32[:, k, b * S:(b + 1) * S]
                                else:
                                    lhs, rhs = w_gu_t[:, w, k, at], n_t16[:, l, k, b * S:(b + 1) * S]
                                ins = pe.matmul(dst, lhs, rhs, start=(k, l) == terms[0], stop=(k, l) == terms[-1])
                        ins.then_inc(hid_filled, 1)
                    elif kind == "down":
                        _, b, m = step
                        n = b * MT + m
                        if wide_branch:
                            pe.wait_ge(h_made, n + 1)
                        else:
                            pe.wait_ge(h_high, n + 1)
                            pe.wait_ge(h_low, n + 1)
                        if m == 0 and b >= 1:
                            pe.wait_ge(y_read, 2 * b)
                        for t in range(QT):
                            dst = ps[:, Y_BANKS[t // 2], (t % 2) * D:(t % 2 + 1) * D]
                            rows = slice(t * P, (t + 1) * P)
                            for l in range(1 if wide_branch else 2):
                                if wide_branch:
                                    lhs, rhs = h32[:, n % NHB, rows], w_d_t32[:, m, :]
                                else:
                                    lhs, rhs = h16[:, n % NHB, l, rows], w_d_t[:, m, :]
                                ins = pe.matmul(dst, lhs, rhs, start=(m == 0 and t % 2 == 0 and l == 0),
                                                stop=(m == MT - 1), skip_group_check=True)
                        ins.then_inc(h_used, 1)

            pe.wait_ge(w_flag_ready, 1)
            wide_w = pe.value_load(w_flag[0:1, 0:1], min_val=0, max_val=1 << 20)
            with pe.If(wide_w > 0):
                ffn_pe(True)
            with pe.Else():
                ffn_pe(False)


_INS = ['x', 'ctx_2048', 'mask_BxS2_ik0', 'g_xattn', 'g_ffn', 'L0_xattn_b', 'L0_ffn_w_gate', 'L0_ffn_w_up',
        'L0_ffn_w_down']
_OUTS = [((4, 512, 256), 'float32')]


def kernel(**inputs):
    import numpy as _np
    import concourse.bacc as _bacc
    from concourse import mybir as _mybir
    from concourse.bass_utils import run_bass_kernel_spmd as _run

    nc = _bacc.Bacc("TRN2", target_bir_lowering=False, num_devices=1)
    arrays, args = {}, []
    for name in _INS:
        a = _np.ascontiguousarray(inputs[name])
        arrays[f"in_{name}_dram"] = a
        args.append(nc.dram_tensor(f"in_{name}_dram", a.shape, _mybir.dt.from_np(a.dtype), kind="ExternalInput").ap())
    for i, (shape, dtype) in enumerate(_OUTS):
        dt = _mybir.dt.from_np(_np.dtype(dtype))
        args.append(nc.dram_tensor(f"out_{i}_dram", shape, dt, kind="ExternalOutput").ap())
    flamingo_block_kernel(nc, *args)
    r = _run(nc, [arrays], core_ids=[0])
    got = tuple(r.results[0][f"out_{i}_dram"] for i in range(len(_OUTS)))
    return got[0]
```

```python
from contextlib import ExitStack

import concourse.bass as bass
from concourse import mybir

F32 = mybir.dt.float32
F16 = mybir.dt.float16
BF16 = mybir.dt.bfloat16
I32 = mybir.dt.int32
ALU = mybir.AluOpType
ACT = mybir.ActivationFunctionType
AX = mybir.AxisListType

P = 128
NH, DH = 8, 32
HG = P // DH
NG = NH // HG
NPART = 3
LN_EPS = 1e-5
MASK_STEP = -1e30
W_SCALE = 1.0 / 127.0
H_SHRINK = 1.0 / 8.0
W_LIMIT = 256.0
K_LIMIT = 60000.0


class WorkRing:

    def __init__(self, banks, emptied_by):
        self.banks, self.emptied_by, self.number, self.who, self.rank = banks, emptied_by, {}, [], []

    def copy(self):
        new = WorkRing(self.banks, self.emptied_by)
        new.number, new.who, new.rank = dict(self.number), list(self.who), list(self.rank)
        return new

    def plan(self, steps, engine_of):
        for step in steps:
            engine = engine_of(step)
            if engine is not None:
                self.number[step] = len(self.who)
                self.who.append(engine)
                self.rank.append(self.who.count(engine))
        return self

    def bank(self, step):
        return self.banks[self.number[step] % len(self.banks)]

    def filled(self, step):
        return self.number[step] + 1

    def emptied(self, step):
        n = self.number[step]
        return self.emptied_by[self.who[n]], self.rank[n]

    def before(self, step):
        n = self.number[step] - len(self.banks)
        return None if n < 0 else (self.emptied_by[self.who[n]], self.rank[n])


def emptied_by_engine(step):
    kind = step[0]
    if kind == "q_stack":
        return "act"
    if kind in ("mask_t", "k_stack", "flag_sum", "row_max", "attn_t", "k_block", "w_flag_sum"):
        return "dve"
    if kind in ("mask_rows", "max_t", "q_wide"):
        return "act"
    if kind == "w_t":
        return "act" if step[1] % 2 else "dve"
    return None


LN_PARTS = ("stats", "norm", "high", "low")


def attention_steps_narrow(B, QT):
    c = 3
    maxima = lambda b: [("row_max", b, c, qt, g) for qt in range(QT) for g in range(NG)]
    steps = [("stats", 1, 2)] + maxima(0) + [("max_split", 0), ("norm", 1, 2), ("max_t", 0)]
    for b in range(B + 1):
        live, q = b < B, b + 2
        ahead = maxima(b + 1) if b + 1 < B else []
        if live:
            steps.append(("scores", b, 0, c, 0))
        if q < B:
            steps += [("high", 1, q), ("low", 1, q)]
        if b >= 2:
            steps.append(("norm", 2, b - 2))
        steps += ahead[0:3]
        if b >= 1:
            steps += [("weigh", b - 1, 1, c), ("o_copy", b - 1, 1)]
        if live:
            steps.append(("scores", b, 0, c, 1))
        if b >= 2:
            steps += [("high", 2, b - 2), ("low", 2, b - 2)]
        steps += ahead[3:6]
        if q < B:
            steps += [("dup", q), ("q_stack", q, 0)]
        if b >= 1:
            steps.append(("attn_t", b - 1, 0))
        if live:
            steps.append(("scores", b, 1, c, 0))
        steps += ahead[6:8]
        if ahead:
            steps.append(("max_split", b + 1))
        if b >= 1:
            steps.append(("attn_t", b - 1, 1))
        if live:
            steps.append(("weigh", b, 0, c))
        if q < B:
            steps.append(("q_stack", q, 1))
        if q + 1 < B:
            steps.append(("stats", 1, q + 1))
        if live:
            steps += [("scores", b, 1, c, 1), ("o_copy", b, 0)]
        if b >= 1:
            steps += [("attn_t", b - 1, 2), ("attn_t", b - 1, 3)]
        if b + 1 < B:
            steps.append(("max_t", b + 1))
        if q < B:
            steps += [("q_stack", q, 2), ("q_stack", q, 3)]
        if q + 1 < B:
            steps.append(("norm", 1, q + 1))
        if b >= 1:
            steps.append(("stats", 2, b - 1))
        if b == B - 2:
            steps.append(("w_check",))
        if b == B - 1:
            steps += [("w_t", i) for i in range(6)] + [("w_flag_sum",)]
    return steps + [(part, 2, B - 1) for part in LN_PARTS[1:]]


def attention_steps_wide(B, QT, NC):
    steps = [(part, 1, b) for b in range(2, B) for part in LN_PARTS]
    for b in range(B):
        steps += [("q_wide", b, g) for g in range(NG)]
        steps += [("k_block", b, c, g) for c in range(NC) for g in range(NG)]
        steps += [("row_max", b, c, qt, g) for c in range(NC) for qt in range(QT) for g in range(NG)]
        steps += [("max_split", b), ("max_t", b)]
        for g in range(NG):
            for c in range(NC):
                steps += [("scores", b, g, c, 0), ("scores", b, g, c, 1), ("weigh", b, g, c)]
            steps.append(("o_copy", b, g))
        steps += [("attn_t", b, qt) for qt in range(QT)] + [(part, 2, b) for part in LN_PARTS]
    return steps + [("w_check",)] + [("w_t", i) for i in range(6)] + [("w_flag_sum",)]


def ffn_steps(B, QT, MT, wide):
    DOWN_LAG = 2
    steps = [("w_wide", i) for i in range(12)] if wide else []
    steps += [("n_t", 0, i) for i in range(QT // 2)]
    for n in range(B * MT + DOWN_LAG):
        b, m = divmod(n, MT)
        if n < B * MT:
            steps.append(("hidden", b, m))
            if m in (2, 3) and b + 1 < B:
                steps.append(("n_t", b + 1, m - 2))
        if n >= DOWN_LAG:
            d, dm = divmod(n - DOWN_LAG, MT)
            steps.append(("down", d, dm))
            if dm == MT - 1:
                steps.append(("finish", d))
    return steps


def flamingo_block_kernel(nc, x, ctx, mask, g_xattn, g_ffn, attn_b, w_gate, w_up, w_down, out):
    B, S, D = x.shape
    SK = ctx.shape[1]
    HID = w_gate.shape[0]
    QT, NC, MT, KD = S // P, SK // P, HID // P, D // P
    LAST = NC - 1
    NT = B * QT
    assert (NH * DH, ctx.shape[2], D, QT, NC) == (D, 2 * D, 256, 4, 4)
    Q_SCALE = float(DH) ** -0.5

    stack = ExitStack()
    with stack:
        def sb(name, shape, dt):
            return stack.enter_context(nc.sbuf_tensor(name, shape, dt))

        def sem(name):
            return stack.enter_context(nc.semaphore(name))

        x_sb = sb("x_sb", [P, NT, D], F32)
        kv = sb("kv", [P, B * NC, 2 * D], F32)
        norm32 = sb("norm32", [P, NT, D], F32)
        norm16 = sb("norm16", [P, 2, NT, D], F16)
        q_stacks = sb("q_stacks", [P, B, NH, S], F16)
        k_stacks = sb("k_stacks", [P, B, NH, P], F16)
        NPB = 4
        probs = sb("probs", [P, NPB, 2 * S], F32)
        o_sb = sb("o_sb", [P, 2, NG + 1, S], F32)
        w_raw = sb("w_raw", [P, 3, MT * D], I32)
        w16 = sb("w16", [P, 3, MT * D], F16)
        w_gu_t = sb("w_gu_t", [P, 2, KD, HID], F16)
        w_d_t = sb("w_d_t", [P, MT, D], F16)
        attn = sb("attn", [P, 2, D], F32)
        ident32 = sb("ident32", [P, P], F32)
        ident16 = sb("ident16", [P, P], F16)
        identb = sb("identb", [P, P], BF16)
        ones32 = sb("ones32", [P, 1], F32)
        sum_cols = sb("sum_cols", [P, NG, DH], F32)
        max_sel = sb("max_sel", [P, NH, P], BF16)
        ones_b = sb("ones_b", [P, P], BF16)
        neg_half = sb("neg_half", [P, QT], F32)
        gates = sb("gates", [P, 3], F32)
        tanh_g = sb("tanh_g", [P, 2], F32)
        y_scale = sb("y_scale", [P, 1], F32)
        NLB = 4
        stats = sb("stats", [P, QT, 6], F32)
        mv = sb("mv", [P, NLB, QT, 2], F32)
        var_eps = sb("var_eps", [P, NLB, QT], F32)
        rstd = sb("rstd", [P, NLB, QT], F32)
        neg_mean = sb("neg_mean", [P, NLB, QT], F32)
        mask_raw = sb("mask_raw", [B * NC, P], I32)
        mask_f = sb("mask_f", [B * NC, P], F32)
        mask_k = sb("mask_k", [P, B * NC], F32)
        key_bias = sb("key_bias", [P, B * NC], F32)
        rest = sb("rest", [P, B * NC], F32)
        bias_parts = sb("bias_parts", [P, B * NC, NPART], BF16)
        bias_rows = sb("bias_rows", [P, B * NC, P], BF16)
        k_abs = sb("k_abs", [P, B], F32)
        checks = sb("checks", [P, B * NC + B], F32)
        verdict = sb("verdict", [1, 4], F32)
        attn_flag = sb("attn_flag", [1, 1], I32)
        w_abs = sb("w_abs", [P, 3], F32)
        w_over = sb("w_over", [P, 1], F32)
        w_flag = sb("w_flag", [1, 1], I32)
        max_c = sb("max_c", [P, QT, NH, NC], F32)
        neg_max = sb("neg_max", [P, QT, NH], F32)
        max_rest = sb("max_rest", [P, QT, NH], F32)
        max_cols = sb("max_cols", [P, QT, P], BF16)
        max_rows = sb("max_rows", [P, 2, S], BF16)
        recip = sb("recip", [P, 2, NH], F32)
        max_parts = max_cols[:, :, 0:NPART * NH].rearrange("p t (a h) -> p t a h", a=NPART)
        q_parts = norm16[:, :, :, :].rearrange("p l t d -> p (l t d)").rearrange(
            "p (n h a l d) -> p n h a l d", n=2 * QT, h=NH, a=2, l=2)
        k_parts = probs[:, :, :].rearrange("p n s -> p (n s)").bitcast(F16)[:, 0:B * NH * P].rearrange(
            "p (b h l a d) -> p b h l a d", b=B, h=NH, l=2, a=2)
        q_mem = q_stacks[:, :, :, :].rearrange("p b h s -> p (b h s)").bitcast(F32)
        k_blocks = q_mem[:, 0:NC * NH * P].rearrange("p (c h k) -> p c h k", c=NC, h=NH)
        q_wide = q_mem[:, NC * NH * P:NC * NH * P + NG * S].rearrange("p (g s) -> p g s", g=NG)
        n_t32 = q_mem[:, 0:KD * NT * P].rearrange("p (k s) -> p k s", k=KD)
        n_t16 = q_stacks[:, :, :, :].rearrange("p b h s -> p (b h s)")[:, 0:2 * KD * NT * P].rearrange(
            "p (l k s) -> p l k s", l=2, k=KD)
        kv_mem = kv[:, :, :].rearrange("p c d -> p (c d)")
        w_gu_t32 = kv_mem[:, 0:2 * KD * HID].rearrange("p (w k h) -> p w k h", w=2, k=KD)
        w_d_t32 = kv_mem[:, 2 * KD * HID:2 * KD * HID + MT * D].rearrange("p (m d) -> p m d", m=MT)
        w32 = kv_mem[:, 2 * KD * HID + MT * D:2 * KD * HID + MT * D + MT * D]
        probs_mem = probs[:, :, :].rearrange("p n s -> p (n s)")
        silu = probs_mem[:, 0:2 * S].rearrange("p (n s) -> p n s", n=2)
        NHB = 4
        h16 = probs_mem[:, 2 * S:2 * S + NHB * S].bitcast(F16).rearrange("p (n l s) -> p n l s", n=NHB, l=2)
        o_mem = o_sb[:, :, :, :].rearrange("p n g s -> p (n g s)")
        h32 = o_mem[:, 0:NHB * S].rearrange("p (n s) -> p n s", n=NHB)

        ps = stack.enter_context(nc.psum_tensor("ps", [P, 8, 512], F32))
        WORK, SCORES, O_BANK, D_BANK = (0, 1), 2, 6, 7

        def bank32(n):
            return ps[:, n, :]

        def bank16(n):
            return ps[:, n, :].bitcast(F16)

        def bankb(n):
            return ps[:, n, :].bitcast(BF16)

        x_loaded = [sem(f"x_loaded{b}") for b in range(B)]
        kv_loaded = [sem(f"kv_loaded{b}") for b in range(B)]
        kv_rest_loaded = sem("kv_rest_loaded")
        mask_loaded, gates_loaded = sem("mask_loaded"), sem("gates_loaded")
        w_loaded = [sem(f"w_loaded{i}") for i in range(3)]
        tanh_ready = sem("tanh_ready")
        pool_done = sem("pool_done")
        CONSTS = 11
        zeros_written = sem("zeros_written")
        dve_done = sem("dve_done")
        mask_cast = sem("mask_cast")
        bias_split = sem("bias_split")
        checks_made = sem("checks_made")
        attn_flag_ready, w_flag_ready = sem("attn_flag_ready"), sem("w_flag_ready")
        w_checked = sem("w_checked")
        key_bias_ready = sem("key_bias_ready")
        k_high, k_low = sem("k_high"), sem("k_low")
        var_ready, rstd_ready = sem("var_ready"), sem("rstd_ready")
        normed = {1: sem("normed_q"), 2: sem("normed_x1")}
        norm_high, norm_low, q_doubled = sem("norm_high"), sem("norm_low"), sem("q_doubled")
        w_cast = sem("w_cast")
        work_filled = sem("work_filled")
        emptied_by = {"dve": sem("work_emptied_dve"), "act": sem("work_emptied_act")}
        max_split = sem("max_split")
        scores_filled, exp_done, weighed = sem("scores_filled"), sem("exp_done"), sem("weighed")
        o_copied = sem("o_copied")
        x1_ready = sem("x1_ready")
        f_filled = sem("f_filled")
        f_emptied = {"dve": sem("f_emptied_dve"), "act": sem("f_emptied_act")}
        w_wide_cast = sem("w_wide_cast")
        hid_filled, silu_done, h_made = sem("hid_filled"), sem("silu_done"), sem("h_made")
        h_high, h_low, h_used = sem("h_high"), sem("h_low"), sem("h_used")
        y_read = sem("y_read")
        stored = sem("stored")

        common = [("stats", 1, 0), ("mask_t",), ("norm", 1, 0), ("high", 1, 0), ("low", 1, 0), ("k_parts",)]
        common += [("flag_sum",), ("stats", 1, 1), ("dup", 0), ("mask_rows", 0), ("mask_rows", 1)]
        common += [("q_stack", 0, 0), ("k_stack", 0), ("norm", 1, 1), ("q_stack", 0, 1), ("k_stack", 1)]
        common += [("high", 1, 1), ("low", 1, 1), ("q_stack", 0, 2), ("k_stack", 2), ("q_stack", 0, 3)]
        common += [("k_stack", 3), ("dup", 1)] + [("q_stack", 1, qt) for qt in range(QT)]
        ring0 = WorkRing(WORK, emptied_by).plan(common, emptied_by_engine)
        narrow_steps = attention_steps_narrow(B, QT)
        wide_steps = attention_steps_wide(B, QT, NC)
        chunks_of = {False: [LAST], True: list(range(NC))}
        plans = {False: (narrow_steps, ring0.copy().plan(narrow_steps, emptied_by_engine)),
                 True: (wide_steps, ring0.copy().plan(wide_steps, emptied_by_engine))}

        def order(steps, kind):
            return {s: n for n, s in enumerate([s for s in steps if s[0] == kind])}

        ln_of = {}
        for w in (False, True):
            for part in LN_PARTS:
                ln_of[w, part] = order(common + plans[w][0], part)

        F_WORK, Y_BANKS = (0, 1), (6, 7)

        def ffn_emptied_by(step):
            if step[0] == "n_t":
                return "act" if step[2] % 2 else "dve"
            return ("act" if step[1] % 2 else "dve") if step[0] == "w_wide" else None

        ffn_rings = {w: WorkRing(F_WORK, f_emptied).plan(ffn_steps(B, QT, MT, w), ffn_emptied_by)
                     for w in (False, True)}

        def normed_out(step, ring, wide_branch):
            _, b, i = step
            s0 = (b * QT + 2 * i) * P
            if wide_branch:
                return (n_t32[:, :, s0:s0 + 2 * P].rearrange("p k (t s) -> p k t s", t=2),
                        bank32(ring.bank(step)).rearrange("p (k t s) -> p k t s", k=KD, t=2))
            return (n_t16[:, :, :, s0:s0 + 2 * P].rearrange("p l k (t s) -> p (l k) t s", t=2),
                    bank16(ring.bank(step)).rearrange("p (k t s) -> p k t s", k=2 * KD, t=2))

        def wide_weights_out(step, ring):
            wh, part = divmod(step[1], 2)
            w, half = divmod(wh, 2)
            M2 = MT // 2
            got = bank32(ring.bank(step))[:, 0:M2 * P].rearrange("p (m k) -> p m k", m=M2)
            if w < 2:
                return (w_gu_t32[:, w, half, part * M2 * P:(part + 1) * M2 * P]
                        .rearrange("p (m k) -> p m k", m=M2), got)
            return w_d_t32[:, part * M2:(part + 1) * M2, half * P:(half + 1) * P], got

        block = stack.enter_context(nc.Block())

        def load_x(eng, b):
            eng.dma_start(x_sb[:, b * QT:(b + 1) * QT, :],
                          x[b].rearrange("(t p) d -> p t d", p=P)).then_inc(x_loaded[b], 16)

        def load_kv(eng, b):
            eng.dma_start(kv[:, b * NC + LAST, :], ctx[b, LAST * P:SK, :]).then_inc(kv_loaded[b], 16)

        @block.sync
        def _(sp):
            load_x(sp, 0)
            for b in range(0, B, 2):
                load_kv(sp, b)
            load_x(sp, 3)
            for i, w in enumerate((w_gate, w_up)):
                sp.dma_start(w_raw[:, i, :].rearrange("p (m d) -> p m d", d=D),
                             w.rearrange("(m p) d -> p m d", p=P)).then_inc(w_loaded[i], 16)
            sp.wait_ge(attn_flag_ready, 1)
            wide = sp.value_load(attn_flag[0:1, 0:1], min_val=0, max_val=1 << 20)
            with sp.If(wide > 0):
                for b in range(B):
                    sp.dma_start(kv[:, b * NC:b * NC + LAST, :],
                                 ctx[b, 0:LAST * P, :].rearrange("(c p) d -> p c d", p=P)
                                 ).then_inc(kv_rest_loaded, 16)
            for b in range(B):
                for half in range(2):
                    sp.wait_ge(y_read, 2 * b + half + 1)
                    t = b * QT + 2 * half
                    sp.dma_start(out[b, 2 * half * P:2 * (half + 1) * P, :].rearrange("(t p) d -> p t d", p=P),
                                 x_sb[:, t:t + 2, :]).then_inc(stored, 16)
            sp.wait_ge(stored, 16 * 2 * B)

        def norm_parts(step):
            _, which, b = step
            t = slice(b * QT, (b + 1) * QT)
            if which == 2:
                return norm32[:, t, :], norm16[:, 0, t, :], norm16[:, 1, t, :]
            full = norm32[:, t, :].rearrange("p t (h d) -> p (t h) d", h=NH)
            r = slice((b % 2) * QT, (b % 2 + 1) * QT)
            return full, *(q_parts[:, r, :, 0, l, :].rearrange("p t h d -> p (t h) d") for l in range(2))

        def key_parts(b):
            full = kv[:, b * NC + LAST, 0:D].rearrange("p (h d) -> p h d", h=NH).unsqueeze(2).to_broadcast(
                (P, NH, 2, DH))
            return full, k_parts[:, b, :, 0, :, :], k_parts[:, b, :, 1, :, :]

        def ln_pool(pool, step, wide_branch):
            kind, which, b = step
            place = ln_of[wide_branch, kind][step]
            if kind == "stats":
                pool.wait_ge(var_ready, place + 1)
                pool.tensor_tensor(rstd[:, place % NLB, :], var_eps[:, place % NLB, :], neg_half[:, :],
                                   ALU.pow).then_inc(rstd_ready, 1)
            elif kind == "norm" and which == 2:
                at = ln_of[wide_branch, "stats"]["stats", which, b]
                pool.wait_ge(rstd_ready, at + 1)
                for i in range(QT):
                    ins = pool.tensor_scalar(norm32[:, b * QT + i, :], x_sb[:, b * QT + i, :],
                                             neg_mean[:, at % NLB, i:i + 1], rstd[:, at % NLB, i:i + 1],
                                             ALU.add, ALU.mult)
                ins.then_inc(normed[2], 1)
            elif kind == "low":
                pool.wait_ge(norm_high, place + 1)
                full, high, low = norm_parts(step)
                pool.tensor_tensor(low, full, high, ALU.subtract).then_inc(norm_low, 1)

        @block.gpsimd
        def _(pool):
            zeroed = (ident32[:, :], ident16[:, :], identb[:, :], sum_cols[:, :, :])
            for n, m in enumerate(zeroed):
                pool.memset(m, 0.0).then_inc(pool_done, 1)
            pool.memset(neg_half[:, :], -0.5).then_inc(pool_done, 1)
            pool.memset(ones32[:, :], 1.0).then_inc(pool_done, 1)
            pool.memset(ones_b[:, :], 1.0).then_inc(pool_done, 1)
            pool.wait_ge(pool_done, 7)
            for n, m in enumerate((ident32, ident16, identb)):
                pool.affine_select(out=m[:, :], in_=m[:, :], compare_op=ALU.not_equal, fill=1.0, base=0,
                                   pattern=[[-1, P]], channel_multiplier=1).then_inc(pool_done, 1)
            pool.affine_select(out=sum_cols[:, :, :], in_=sum_cols[:, :, :], compare_op=ALU.not_equal, fill=1.0,
                               base=0, pattern=[[-1, NG], [1, DH]], channel_multiplier=0).then_inc(pool_done, 1)

            def max_selector():
                for part in range(NPART):
                    pool.wait_ge(zeros_written, 1) if part == 0 else pool.wait_ge(pool_done, CONSTS + part)
                    pool.affine_select(out=max_sel[:, :, :], in_=max_sel[:, :, :], compare_op=ALU.not_equal,
                                       fill=1.0, base=-NH * part, pattern=[[-1, NH], [0, P]],
                                       channel_multiplier=1).then_inc(pool_done, 1)

            for step in common:
                if step[0] in LN_PARTS:
                    ln_pool(pool, step, False)
                if step[0] == "k_parts":
                    for b in range(B):
                        pool.wait_ge(k_high, b + 1)
                        full, high, low = key_parts(b)
                        pool.tensor_tensor(low, full, high, ALU.subtract).then_inc(k_low, 1)
            max_selector()

            def attention_pool(wide_branch):
                steps, ring = plans[wide_branch]
                place = order(steps, "attn_t")
                for step in steps:
                    if step[0] in LN_PARTS:
                        ln_pool(pool, step, wide_branch)
                    elif step[0] == "attn_t":
                        n = place[step]
                        t = step[1] * QT + step[2]
                        pool.wait_ge(*ring.emptied(step))
                        pool.tensor_tensor(x_sb[:, t, :], x_sb[:, t, :], attn[:, n % 2, :],
                                           ALU.add).then_inc(x1_ready, 1)

            pool.wait_ge(attn_flag_ready, 1)
            wide = pool.value_load(attn_flag[0:1, 0:1], min_val=0, max_val=1 << 20)
            with pool.If(wide > 0):
                attention_pool(True)
            with pool.Else():
                attention_pool(False)

        def ln_act(act, step, wide_branch):
            _, which, b = step
            act.wait_ge(normed[which], b + 1)
            if which == 1 and b >= 2:
                act.wait_ge(work_filled, ring0.filled(("q_stack", b - 2, QT - 1)))
            full, high, _ = norm_parts(step)
            act.activation(high, full, ACT.Copy).then_inc(norm_high, 1)

        def q_stack_out(step, ring):
            _, b, qt = step
            return (q_stacks[:, b, :, qt * P:(qt + 1) * P],
                    bank16(ring.bank(step)).rearrange("p (h k) -> p h k", h=NH))

        def weights_out(step, ring):
            w, half = divmod(step[1], 2)
            got = bank16(ring.bank(step))[:, 0:MT * P].rearrange("p (m k) -> p m k", m=MT)
            if w < 2:
                return w_gu_t[:, w, half, :].rearrange("p (m k) -> p m k", m=MT), got
            return w_d_t[:, :, half * P:(half + 1) * P], got

        @block.scalar
        def _(act):
            act.dma_start(mask_raw[:, :], mask.rearrange("b (c k) -> (b c) k", k=P)).then_inc(mask_loaded, 16)
            for n, g in enumerate((g_xattn, g_ffn, attn_b)):
                act.dma_start(gates[:, n:n + 1], g.partition_broadcast(P)).then_inc(gates_loaded, 16)
            load_x(act, 1)
            for b in range(1, B, 2):
                load_kv(act, b)
            load_x(act, 2)
            act.dma_start(w_raw[:, 2, :].rearrange("p (t h) -> p t h", h=HID),
                          w_down.rearrange("(t p) h -> p t h", p=P)).then_inc(w_loaded[2], 16)
            act.wait_ge(gates_loaded, 48)
            act.activation(tanh_g[:, :], gates[:, 0:2], ACT.Tanh).then_inc(tanh_ready, 1)

            def mask_rows_copy(step, ring):
                half = step[1]
                act.wait_ge(zeros_written, 1)
                act.wait_ge(work_filled, ring.filled(step))
                per = B * NC // 2
                act.activation(bias_rows[0:NPART, half * per:(half + 1) * per, :],
                               bankb(ring.bank(step))[0:NPART, :].rearrange("p (c k) -> p c k", k=P),
                               ACT.Copy).then_inc(emptied_by["act"], 1)

            for step in common:
                if step[0] == "high":
                    ln_act(act, step, False)
                if step[0] == "mask_rows":
                    mask_rows_copy(step, ring0)
                if step[0] == "q_stack" and emptied_by_engine(step) == "act":
                    act.wait_ge(work_filled, ring0.filled(step))
                    act.activation(*q_stack_out(step, ring0), ACT.Copy).then_inc(emptied_by["act"], 1)

            def attention_act(wide_branch):
                steps, ring = plans[wide_branch]
                pair_of, unit_of = order(steps, "scores"), order(steps, "weigh")
                act.wait_ge(key_bias_ready, 1)
                for step in steps:
                    kind = step[0]
                    if kind == "high":
                        ln_act(act, step, wide_branch)
                    elif kind in ("q_stack", "w_t") and emptied_by_engine(step) == "act":
                        act.wait_ge(work_filled, ring.filled(step))
                        dst, src = q_stack_out(step, ring) if kind == "q_stack" else weights_out(step, ring)
                        act.activation(dst, src, ACT.Copy).then_inc(emptied_by["act"], 1)
                    elif kind == "q_wide":
                        act.wait_ge(work_filled, ring.filled(step))
                        act.activation(q_wide[:, step[2], :], bank32(ring.bank(step)),
                                       ACT.Copy).then_inc(emptied_by["act"], 1)
                    elif kind == "max_t":
                        act.wait_ge(work_filled, ring.filled(step))
                        act.activation(max_rows[:, step[1] % 2, :], bankb(ring.bank(step))[:, 0:S],
                                       ACT.Copy).then_inc(emptied_by["act"], 1)
                    elif kind == "scores":
                        _, b, g, c, _ = step
                        j = pair_of[step]
                        act.wait_ge(scores_filled, j + 1)
                        if j >= NPB:
                            act.wait_ge(weighed, (j - NPB) // 2 + 1)
                        n = b * NC + c
                        act.activation(probs[:, j % NPB, :],
                                       ps[:, SCORES + 2 * (j % 2):SCORES + 2 * (j % 2) + 2, :], ACT.Exp,
                                       bias=key_bias[:, n:n + 1]).then_inc(exp_done, 1)
                    elif kind == "o_copy":
                        _, b, g = step
                        act.wait_ge(weighed, unit_of[("weigh", b, g, chunks_of[wide_branch][-1])] + 1)
                        if b >= 2 and g == 0:
                            act.wait_ge(work_filled, ring.filled(("attn_t", b - 2, QT - 1)))
                        act.activation(o_sb[:, b % 2, g, :], bank32(O_BANK), ACT.Copy).then_inc(o_copied, 1)
                        if g == NG - 1:
                            act.activation(o_sb[:, b % 2, NG, :], bank32(D_BANK), ACT.Copy).then_inc(o_copied, 1)

            act.wait_ge(attn_flag_ready, 1)
            wide = act.value_load(attn_flag[0:1, 0:1], min_val=0, max_val=1 << 20)
            with act.If(wide > 0):
                attention_act(True)
            with act.Else():
                attention_act(False)

            def ffn_act(wide_branch):
                steps = ffn_steps(B, QT, MT, wide_branch)
                ring = ffn_rings[wide_branch]
                for step in steps:
                    kind = step[0]
                    if kind in ("n_t", "w_wide") and ffn_emptied_by(step) == "act":
                        act.wait_ge(f_filled, ring.filled(step))
                        if kind == "n_t":
                            dst, src = normed_out(step, ring, wide_branch)
                        else:
                            dst, src = wide_weights_out(step, ring)
                        act.activation(dst, src, ACT.Copy).then_inc(f_emptied["act"], 1)
                    elif kind == "hidden":
                        n = step[1] * MT + step[2]
                        act.wait_ge(hid_filled, n + 1)
                        if n >= 2:
                            act.wait_ge(h_made, n - 1)
                        act.activation(silu[:, n % 2, :], bank32(SCORES + 2 * (n % 2)), ACT.Silu,
                                       scale=W_SCALE).then_inc(silu_done, 1)
                        if n >= 1 and not wide_branch:
                            high_part(n - 1)
                if not wide_branch:
                    high_part(B * MT - 1)

            def high_part(n):
                act.wait_ge(h_made, n + 1)
                if n >= NHB:
                    act.wait_ge(h_used, n - NHB + 1)
                act.activation(h16[:, n % NHB, 0, :], h32[:, n % NHB, :], ACT.Copy).then_inc(h_high, 1)

            act.wait_ge(w_flag_ready, 1)
            wide_w = act.value_load(w_flag[0:1, 0:1], min_val=0, max_val=1 << 20)
            with act.If(wide_w > 0):
                ffn_act(True)
            with act.Else():
                ffn_act(False)

        @block.vector
        def _(dve):
            count = [0]

            def mine(ins):
                ins.then_inc(dve_done, 1)
                count[0] += 1

            def wait_mine():
                dve.wait_ge(dve_done, count[0])

            def ln_dve(step, wide_branch):
                kind, which, b = step
                t0 = b * QT
                if kind == "stats":
                    place = ln_of[wide_branch, kind][step]
                    if which == 1:
                        dve.wait_ge(x_loaded[b], 16)
                    else:
                        dve.wait_ge(x1_ready, QT * (b + 1))
                    if place >= NLB:
                        if place - NLB < B:
                            dve.wait_ge(normed[1], place - NLB + 1)
                        else:
                            dve.wait_ge(normed[2], place - NLB - B + 1)
                    for i in range(QT):
                        mine(dve.bn_stats(stats[:, i, :], x_sb[:, t0 + i, :]))
                    wait_mine()
                    for i in range(QT):
                        mine(dve.bn_aggr(mv[:, place % NLB, i, :], stats[:, i, :]))
                    wait_mine()
                    if which == 2:
                        mine(dve.tensor_scalar(neg_mean[:, place % NLB, :], mv[:, place % NLB, :, 0], -1.0, None,
                                               ALU.mult))
                        wait_mine()
                    dve.tensor_scalar(var_eps[:, place % NLB, :], mv[:, place % NLB, :, 1], LN_EPS,
                                      float(DH) if which == 1 else 1.0, ALU.add, ALU.mult).then_inc(var_ready, 1)
                elif kind == "norm" and which == 1:
                    at = ln_of[wide_branch, "stats"]["stats", which, b]
                    dve.wait_ge(rstd_ready, at + 1)
                    for i in range(QT):
                        ins = dve.tensor_scalar(norm32[:, t0 + i, :], x_sb[:, t0 + i, :],
                                                mv[:, at % NLB, i, 0:1], rstd[:, at % NLB, i:i + 1],
                                                ALU.subtract, ALU.mult)
                    ins.then_inc(normed[1], 1)

            def double_q(b, wide_branch):
                dve.wait_ge(norm_low, ln_of[wide_branch, "low"]["low", 1, b] + 1)
                r = slice((b % 2) * QT, (b % 2 + 1) * QT)
                src, dst = (q_parts[:, r, :, a, :, :].rearrange("p t h l d -> p (t h) (l d)") for a in range(2))
                dve.tensor_copy(dst, src).then_inc(q_doubled, 1)

            def mask_steps():
                dve.wait_ge(mask_loaded, 16)
                dve.tensor_copy(mask_f[:, :], mask_raw[:, :]).then_inc(mask_cast, 1)
                step = ("mask_t",)
                dve.wait_ge(work_filled, ring0.filled(step))
                dve.tensor_copy(mask_k[:, :], bank32(ring0.bank(step))[:, 0:B * NC]).then_inc(emptied_by["dve"], 1)
                dve.wait_ge(*ring0.emptied(step))
                mine(dve.tensor_scalar(key_bias[:, :], mask_k[:, :], -1.0, 1.0, ALU.mult, ALU.add))
                mine(dve.tensor_scalar(checks[:, 0:B * NC], mask_k[:, :], 0.0, None, ALU.not_equal))
                last = mask_k[:, :].rearrange("p (b c) -> p b c", c=NC)[:, :, LAST]
                mine(dve.tensor_scalar(checks[:, B * NC:B * NC + B], last, 1.0, None, ALU.is_ge))
                wait_mine()
                dve.wait_ge(gates_loaded, 48)
                mine(dve.tensor_scalar(key_bias[:, :], key_bias[:, :], MASK_STEP, gates[:, 2:3], ALU.mult, ALU.add))
                wait_mine()
                dve.tensor_scalar(key_bias[:, :], key_bias[:, :], 3e38, -3e38, ALU.min, ALU.max
                                  ).then_inc(key_bias_ready, 1)
                dve.wait_ge(key_bias_ready, 1)
                mine(dve.tensor_copy(bias_parts[:, :, 0], key_bias[:, :]))
                wait_mine()
                mine(dve.tensor_tensor(rest[:, :], key_bias[:, :], bias_parts[:, :, 0], ALU.subtract))
                wait_mine()
                mine(dve.tensor_copy(bias_parts[:, :, 1], rest[:, :]))
                wait_mine()
                dve.tensor_tensor(bias_parts[:, :, 2], rest[:, :], bias_parts[:, :, 1], ALU.subtract
                                  ).then_inc(bias_split, 1)

            def key_checks():
                for b in range(B):
                    dve.wait_ge(kv_loaded[b], 16)
                    mine(dve.tensor_reduce(k_abs[:, b:b + 1], kv[:, b * NC + LAST, 0:D], AX.X, ALU.max,
                                           apply_absolute_value=True))
                    full, high, _ = key_parts(b)
                    dve.tensor_scalar(high, full, K_LIMIT, -K_LIMIT, ALU.min, ALU.max).then_inc(k_high, 1)
                wait_mine()
                slot = checks[:, 0:B * NC].rearrange("p (b c) -> p b c", c=NC)[:, :, LAST]
                dve.tensor_scalar(slot, k_abs[:, :], K_LIMIT, None, ALU.is_gt).then_inc(checks_made, 1)

            def attn_verdict():
                step = ("flag_sum",)
                dve.wait_ge(work_filled, ring0.filled(step))
                counts = bank32(ring0.bank(step))
                mine(dve.tensor_reduce(verdict[:, 0:1], counts[0:1, 0:B * NC], AX.X, ALU.add))
                dve.tensor_reduce(verdict[:, 1:2], counts[0:1, B * NC:B * NC + B], AX.X, ALU.min
                                  ).then_inc(emptied_by["dve"], 1)
                wait_mine()
                dve.wait_ge(*ring0.emptied(step))
                dve.scalar_tensor_tensor(out=attn_flag[:, :], in0=verdict[:, 1:2], scalar=1.0,
                                         in1=verdict[:, 0:1], op0=ALU.is_lt, op1=ALU.add
                                         ).then_inc(attn_flag_ready, 1)

            for m in (max_sel[:, :, :].rearrange("p h k -> p (h k)"), max_cols[:, :, :].rearrange("p t k -> p (t k)"),
                      bias_rows[:, :, :].rearrange("p c k -> p (c k)")):
                ins = dve.memset(m.bitcast(F32), 0.0)
            ins.then_inc(zeros_written, 1)
            for step in common:
                if step[0] in LN_PARTS:
                    ln_dve(step, False)
                elif step[0] == "mask_t":
                    mask_steps()
                elif step[0] == "k_parts":
                    key_checks()
                elif step[0] == "dup":
                    double_q(step[1], False)
                elif step[0] == "flag_sum":
                    attn_verdict()
                elif step[0] == "q_stack" and emptied_by_engine(step) == "dve":
                    dve.wait_ge(work_filled, ring0.filled(step))
                    dve.tensor_copy(*q_stack_out(step, ring0)).then_inc(emptied_by["dve"], 1)
                elif step[0] == "k_stack":
                    dve.wait_ge(work_filled, ring0.filled(step))
                    dve.tensor_copy(k_stacks[:, step[1], :, :],
                                    bank16(ring0.bank(step)).rearrange("p (h k) -> p h k", h=NH)
                                    ).then_inc(emptied_by["dve"], 1)
            dve.wait_ge(tanh_ready, 1)
            mine(dve.tensor_scalar(y_scale[:, :], tanh_g[:, 1:2], W_SCALE / H_SHRINK, None, ALU.mult))
            wait_mine()

            def attention_dve(wide_branch):
                steps, ring = plans[wide_branch]
                chunks = chunks_of[wide_branch]
                attn_of = order(steps, "attn_t")
                if wide_branch:
                    for b in range(2):
                        for qt in range(QT):
                            dve.wait_ge(*ring.emptied(("q_stack", b, qt)))
                    mine(dve.memset(k_blocks, 0.0))
                    wait_mine()
                for step in steps:
                    kind = step[0]
                    if kind in LN_PARTS:
                        ln_dve(step, wide_branch)
                    elif kind == "dup":
                        double_q(step[1], wide_branch)
                    elif kind in ("q_stack", "w_t") and emptied_by_engine(step) == "dve":
                        dve.wait_ge(work_filled, ring.filled(step))
                        dst, src = q_stack_out(step, ring) if kind == "q_stack" else weights_out(step, ring)
                        dve.tensor_copy(dst, src).then_inc(emptied_by["dve"], 1)
                    elif kind == "k_block":
                        _, b, c, g = step
                        dve.wait_ge(work_filled, ring.filled(step))
                        for j in range(HG):
                            rows = slice(j * DH, (j + 1) * DH)
                            ins = dve.tensor_copy(k_blocks[rows, c, g * HG + j, :],
                                                  bank32(ring.bank(step))[rows, 0:P])
                        ins.then_inc(emptied_by["dve"], 1)
                    elif kind == "row_max":
                        _, b, c, qt, g = step
                        dve.wait_ge(work_filled, ring.filled(step))
                        if qt == 0 and g == 0 and c == chunks[0] and b >= 1:
                            dve.wait_ge(max_split, b)
                        one = len(chunks) == 1
                        dst = neg_max[:, qt, g * HG:(g + 1) * HG] if one else max_c[:, qt, g * HG:(g + 1) * HG, c]
                        dve.tensor_reduce(dst, bank32(ring.bank(step)).rearrange("p (h k) -> p h k", h=HG),
                                          AX.X, ALU.max, negate=one).then_inc(emptied_by["dve"], 1)
                    elif kind == "max_split":
                        b = step[1]
                        dve.wait_ge(*ring.emptied(("row_max", b, chunks[-1], QT - 1, NG - 1)))
                        if b >= 1:
                            dve.wait_ge(work_filled, ring.filled(("max_t", b - 1)))
                        if len(chunks) > 1:
                            mine(dve.tensor_reduce(neg_max[:, :, :], max_c[:, :, :, :], AX.X, ALU.max, negate=True))
                            wait_mine()
                        mine(dve.tensor_copy(max_parts[:, :, 0, :], neg_max[:, :, :]))
                        wait_mine()
                        mine(dve.tensor_tensor(max_rest[:, :, :], neg_max[:, :, :], max_parts[:, :, 0, :],
                                               ALU.subtract))
                        wait_mine()
                        mine(dve.tensor_copy(max_parts[:, :, 1, :], max_rest[:, :, :]))
                        wait_mine()
                        dve.tensor_tensor(max_parts[:, :, 2, :], max_rest[:, :, :], max_parts[:, :, 1, :],
                                          ALU.subtract).then_inc(max_split, 1)
                    elif kind == "attn_t":
                        _, b, qt = step
                        n = attn_of[step]
                        got = bank32(ring.bank(step))
                        dve.wait_ge(work_filled, ring.filled(step))
                        if n >= 2:
                            dve.wait_ge(x1_ready, n - 1)
                        sums = got[:, NG * P:(NG + 1) * P].rearrange("p (j d) -> p d j", d=DH)[:, 0:NG, :]
                        mine(dve.reciprocal(recip[:, n % 2, :].rearrange("p (g j) -> p g j", g=NG), sums))
                        wait_mine()
                        dve.scalar_tensor_tensor(
                            out=attn[:, n % 2, :].rearrange("p (h d) -> p h d", d=DH),
                            in0=got[:, 0:NG * P].rearrange("p (h d) -> p h d", d=DH), scalar=tanh_g[:, 0:1],
                            in1=recip[:, n % 2, :].unsqueeze(2).to_broadcast((P, NH, DH)),
                            op0=ALU.mult, op1=ALU.mult).then_inc(emptied_by["dve"], 1)
                    elif kind == "w_check":
                        for i in range(3):
                            dve.wait_ge(w_loaded[i], 16)
                            dve.tensor_scalar(w16[:, i, :], w_raw[:, i, :], W_LIMIT, -W_LIMIT, ALU.min, ALU.max
                                              ).then_inc(w_cast, 1)
                        for i in range(3):
                            dve.wait_ge(w_loaded[i], 16)
                            mine(dve.tensor_reduce(w_abs[:, i:i + 1], w_raw[:, i, :], AX.X, ALU.max,
                                                   apply_absolute_value=True))
                        wait_mine()
                        mine(dve.tensor_reduce(w_over[:, :], w_abs[:, :], AX.X, ALU.max))
                        wait_mine()
                        dve.tensor_scalar(w_over[:, :], w_over[:, :], W_LIMIT, None, ALU.is_gt).then_inc(w_checked, 1)
                    elif kind == "w_flag_sum":
                        dve.wait_ge(work_filled, ring.filled(step))
                        dve.tensor_copy(verdict[:, 2:3], bank32(ring.bank(step))[0:1, 0:1]
                                        ).then_inc(emptied_by["dve"], 1)
                        dve.wait_ge(*ring.emptied(step))
                        dve.tensor_copy(w_flag[:, :], verdict[:, 2:3]).then_inc(w_flag_ready, 1)

            dve.wait_ge(attn_flag_ready, 1)
            wide = dve.value_load(attn_flag[0:1, 0:1], min_val=0, max_val=1 << 20)
            at_branch = count[0]
            with dve.If(wide > 0):
                attention_dve(True)
            count[0] = at_branch
            with dve.Else():
                attention_dve(False)

            def ffn_dve(wide_branch):
                ring = ffn_rings[wide_branch]
                steps = ffn_steps(B, QT, MT, wide_branch)
                for step in steps:
                    kind = step[0]
                    if kind == "w_wide" and step[1] % 4 == 0:
                        if step[1]:
                            dve.wait_ge(f_filled, ring.filled(("w_wide", step[1] - 1)))
                        dve.tensor_copy(w32, w_raw[:, step[1] // 4, :]).then_inc(w_wide_cast, 1)
                    if kind in ("n_t", "w_wide") and ffn_emptied_by(step) == "dve":
                        dve.wait_ge(f_filled, ring.filled(step))
                        if kind == "n_t":
                            dst, src = normed_out(step, ring, wide_branch)
                        else:
                            dst, src = wide_weights_out(step, ring)
                        dve.tensor_copy(dst, src).then_inc(f_emptied["dve"], 1)
                    elif kind == "hidden":
                        n = step[1] * MT + step[2]
                        dve.wait_ge(silu_done, n + 1)
                        if n >= NHB:
                            dve.wait_ge(h_used, n - NHB + 1)
                        dve.scalar_tensor_tensor(out=h32[:, n % NHB, :], in0=bank32(SCORES + 2 * (n % 2) + 1),
                                                 scalar=W_SCALE * H_SHRINK, in1=silu[:, n % 2, :],
                                                 op0=ALU.mult, op1=ALU.mult).then_inc(h_made, 1)
                        if n >= 1 and not wide_branch:
                            low_part(n - 1)
                        if n == B * MT - 1 and not wide_branch:
                            low_part(n)
                    elif kind == "finish":
                        b = step[1]
                        for half in range(2):
                            for i in range(2):
                                t = b * QT + 2 * half + i
                                dve.wait_ge(h_used, MT * (b + 1))
                                ins = dve.scalar_tensor_tensor(
                                    out=x_sb[:, t, :], in0=ps[:, Y_BANKS[half], i * D:(i + 1) * D],
                                    scalar=y_scale[:, 0:1], in1=x_sb[:, t, :], op0=ALU.mult, op1=ALU.add)
                            ins.then_inc(y_read, 1)

            def low_part(n):
                dve.wait_ge(h_high, n + 1)
                dve.tensor_tensor(h16[:, n % NHB, 1, :], h32[:, n % NHB, :], h16[:, n % NHB, 0, :],
                                  ALU.subtract).then_inc(h_low, 1)

            dve.wait_ge(w_flag_ready, 1)
            wide_w = dve.value_load(w_flag[0:1, 0:1], min_val=0, max_val=1 << 20)
            with dve.If(wide_w > 0):
                ffn_dve(True)
            with dve.Else():
                ffn_dve(False)

        @block.tensor
        def _(pe):
            pe.wait_ge(pool_done, CONSTS)

            def open_work(step, ring):
                last = ring.before(step)
                if last is not None:
                    pe.wait_ge(*last)
                return ring.bank(step)

            def stack_q(step, ring):
                _, b, qt = step
                n = open_work(step, ring)
                pe.wait_ge(q_doubled, b + 1)
                for h in range(NH):
                    src = q_parts[:, (b % 2) * QT + qt, h, :, :, :].rearrange("p a l d -> p (a l d)")
                    ins = pe.transpose(bank16(n)[:, h * P:(h + 1) * P], src, ident16[:, :])
                ins.then_inc(work_filled, 1)

            for step in common:
                kind = step[0]
                if kind == "mask_t":
                    n = open_work(step, ring0)
                    pe.wait_ge(mask_cast, 1)
                    pe.transpose(bank32(n)[:, 0:B * NC], mask_f[:, :], ident32[0:B * NC, 0:B * NC]
                                 ).then_inc(work_filled, 1)
                elif kind == "flag_sum":
                    n = open_work(step, ring0)
                    pe.wait_ge(checks_made, 1)
                    pe.matmul(bank32(n)[0:1, 0:B * NC + B], ones32[:, 0:1], checks[:, :], start=True, stop=True
                              ).then_inc(work_filled, 1)
                elif kind == "mask_rows":
                    n = open_work(step, ring0)
                    pe.wait_ge(bias_split, 1)
                    per = B * NC // 2
                    for i in range(per):
                        ins = pe.transpose(bankb(n)[0:NPART, i * P:(i + 1) * P],
                                           bias_parts[:, step[1] * per + i, :], identb[:, :])
                    ins.then_inc(work_filled, 1)
                elif kind == "q_stack":
                    stack_q(step, ring0)
                elif kind == "k_stack":
                    b = step[1]
                    n = open_work(step, ring0)
                    pe.wait_ge(k_high, b + 1)
                    pe.wait_ge(k_low, b + 1)
                    for h in range(NH):
                        src = k_parts[:, b, h, :, :, :].rearrange("p l a d -> p (l a d)")
                        ins = pe.transpose(bank16(n)[:, h * P:(h + 1) * P], src, ident16[:, :])
                    ins.then_inc(work_filled, 1)

            def attention_pe(wide_branch):
                steps, ring = plans[wide_branch]
                chunks = chunks_of[wide_branch]
                pair_of, unit_of = order(steps, "scores"), order(steps, "weigh")
                pe.wait_ge(*ring.emptied(("mask_rows", 1)))
                pe.wait_ge(pool_done, CONSTS + NPART)
                for step in steps:
                    kind = step[0]
                    if kind == "q_stack":
                        stack_q(step, ring)
                    elif kind == "q_wide":
                        _, b, g = step
                        n = open_work(step, ring)
                        pe.wait_ge(normed[1], b + 1)
                        for qt in range(QT):
                            ins = pe.transpose(bank32(n)[:, qt * P:(qt + 1) * P],
                                               norm32[:, b * QT + qt, g * P:(g + 1) * P], ident32[:, :])
                        ins.then_inc(work_filled, 1)
                    elif kind == "k_block":
                        _, b, c, g = step
                        n = open_work(step, ring)
                        pe.wait_ge(kv_rest_loaded, 16 * B)
                        pe.wait_ge(kv_loaded[b], 16)
                        pe.transpose(bank32(n)[:, 0:P], kv[:, b * NC + c, g * P:(g + 1) * P], ident32[:, :]
                                     ).then_inc(work_filled, 1)
                    elif kind == "row_max":
                        _, b, c, qt, g = step
                        n = open_work(step, ring)
                        if wide_branch:
                            pe.wait_ge(*ring.emptied(("q_wide", b, g)))
                            pe.wait_ge(*ring.emptied(("k_block", b, c, g)))
                            pe.matmul(bank32(n), q_wide[:, g, qt * P:(qt + 1) * P],
                                      k_blocks[:, c, g * HG:(g + 1) * HG, :], start=True, stop=False,
                                      skip_group_check=True)
                        else:
                            pe.wait_ge(*ring.emptied(("q_stack", b, qt)))
                            pe.wait_ge(*ring.emptied(("k_stack", b)))
                            for j in range(HG):
                                h = g * HG + j
                                pe.matmul(bank32(n)[:, j * P:(j + 1) * P], q_stacks[:, b, h, qt * P:(qt + 1) * P],
                                          k_stacks[:, b, h, :], start=(j == 0), stop=False, skip_group_check=True)
                        rows = bias_rows[:, b * NC + c, :].unsqueeze(1).to_broadcast((P, HG, P))
                        pe.matmul(bank32(n), ones_b[:, :], rows, start=False, stop=True, skip_group_check=True
                                  ).then_inc(work_filled, 1)
                    elif kind == "max_t":
                        n = open_work(step, ring)
                        pe.wait_ge(max_split, step[1] + 1)
                        for qt in range(QT):
                            ins = pe.transpose(bankb(n)[:, qt * P:(qt + 1) * P], max_cols[:, qt, :], identb[:, :])
                        ins.then_inc(work_filled, 1)
                    elif kind == "scores":
                        _, b, g, c, pair = step
                        j = pair_of[step]
                        if j >= 2:
                            pe.wait_ge(exp_done, j - 1)
                        pe.wait_ge(*ring.emptied(("max_t", b)))
                        if not wide_branch and pair == 0 and g == 0:
                            for qt in range(QT):
                                pe.wait_ge(*ring.emptied(("q_stack", b, qt)))
                        for i in range(2):
                            h = g * HG + 2 * pair + i
                            dst = bank32(SCORES + 2 * (j % 2) + i)
                            if wide_branch:
                                pe.matmul(dst, k_blocks[:, c, h, :], q_wide[:, g, :], start=True, stop=False)
                            else:
                                pe.matmul(dst, k_stacks[:, b, h, :], q_stacks[:, b, h, :], start=True, stop=False)
                            ins = pe.matmul(dst, max_sel[:, h, :], max_rows[:, b % 2, :], start=False, stop=True)
                        ins.then_inc(scores_filled, 1)
                    elif kind == "weigh":
                        _, b, g, c = step
                        u = unit_of[step]
                        first, last = c == chunks[0], c == chunks[-1]
                        pe.wait_ge(exp_done, 2 * u + 2)
                        copies = b * (NG + 1)
                        if first and copies + g > 0:
                            pe.wait_ge(o_copied, copies + g)
                        for j in range(HG):
                            h = g * HG + j
                            part = slice(j * DH, (j + 1) * DH)
                            pr = probs[:, (2 * u + j // 2) % NPB, (j % 2) * S:(j % 2 + 1) * S]
                            pe.matmul(ps[part, O_BANK, :], kv[:, b * NC + c, D + h * DH:D + (h + 1) * DH], pr,
                                      start=first, stop=last, tile_position=(0, j * DH))
                        for j in range(HG):
                            part = slice(j * DH, (j + 1) * DH)
                            pr = probs[:, (2 * u + j // 2) % NPB, (j % 2) * S:(j % 2 + 1) * S]
                            ins = pe.matmul(ps[part, D_BANK, :], sum_cols[:, g, :], pr,
                                            start=(first and g == 0), stop=(last and g == NG - 1),
                                            tile_position=(0, j * DH))
                        ins.then_inc(weighed, 1)
                    elif kind == "attn_t":
                        _, b, qt = step
                        n = open_work(step, ring)
                        pe.wait_ge(o_copied, (b + 1) * (NG + 1))
                        for g in range(NG + 1):
                            ins = pe.transpose(bank32(n)[:, g * P:(g + 1) * P],
                                               o_sb[:, b % 2, g, qt * P:(qt + 1) * P], ident32[:, :])
                        ins.then_inc(work_filled, 1)
                    elif kind == "w_flag_sum":
                        n = open_work(step, ring)
                        pe.wait_ge(w_checked, 1)
                        pe.matmul(bank32(n)[0:1, 0:1], ones32[:, 0:1], w_over[:, :], start=True, stop=True
                                  ).then_inc(work_filled, 1)
                    elif kind == "w_t":
                        w, half = divmod(step[1], 2)
                        n = open_work(step, ring)
                        pe.wait_ge(w_cast, w + 1)
                        for m in range(MT):
                            at = m * D + half * P if w < 2 else half * HID + m * P
                            ins = pe.transpose(bank16(n)[:, m * P:(m + 1) * P], w16[:, w, at:at + P], ident16[:, :])
                        ins.then_inc(work_filled, 1)

                pe.wait_ge(exp_done, len(pair_of))
                pe.wait_ge(o_copied, B * (NG + 1))
                for engine in emptied_by:
                    pe.wait_ge(emptied_by[engine], ring.who.count(engine))

            pe.wait_ge(attn_flag_ready, 1)
            wide = pe.value_load(attn_flag[0:1, 0:1], min_val=0, max_val=1 << 20)
            with pe.If(wide > 0):
                attention_pe(True)
            with pe.Else():
                attention_pe(False)

            def ffn_pe(wide_branch):
                ring = ffn_rings[wide_branch]
                steps = ffn_steps(B, QT, MT, wide_branch)
                for step in steps:
                    kind = step[0]
                    if kind == "w_wide":
                        wh, part = divmod(step[1], 2)
                        w, half = divmod(wh, 2)
                        n = open_work(step, ring)
                        pe.wait_ge(w_wide_cast, w + 1)
                        for i in range(MT // 2):
                            m = part * (MT // 2) + i
                            at = m * D + half * P if w < 2 else half * HID + m * P
                            ins = pe.transpose(bank32(n)[:, i * P:(i + 1) * P], w32[:, at:at + P], ident32[:, :])
                        ins.then_inc(f_filled, 1)
                    elif kind == "n_t":
                        _, b, i = step
                        n = open_work(step, ring)
                        pe.wait_ge(normed[2], b + 1)
                        pe.wait_ge(norm_high, B + b + 1)
                        pe.wait_ge(norm_low, B + b + 1)
                        for lk in range(KD if wide_branch else 2 * KD):
                            for t in range(2):
                                tile = b * QT + 2 * i + t
                                at = slice((2 * lk + t) * P, (2 * lk + t + 1) * P)
                                l, k = divmod(lk, KD)
                                if wide_branch:
                                    ins = pe.transpose(bank32(n)[:, at], norm32[:, tile, k * P:(k + 1) * P],
                                                       ident32[:, :])
                                else:
                                    ins = pe.transpose(bank16(n)[:, at], norm16[:, l, tile, k * P:(k + 1) * P],
                                                       ident16[:, :])
                        ins.then_inc(f_filled, 1)
                    elif kind == "hidden":
                        _, b, m = step
                        n = b * MT + m
                        if m == 0:
                            for i in range(QT // 2):
                                pe.wait_ge(*ring.emptied(("n_t", b, i)))
                            if n == 0 and wide_branch:
                                for i in range(12):
                                    pe.wait_ge(*ring.emptied(("w_wide", i)))
                        if n >= 2:
                            pe.wait_ge(h_made, n - 1)
                        for w in range(2):
                            dst = bank32(SCORES + 2 * (n % 2) + w)
                            terms = [(k, l) for k in range(KD) for l in range(1 if wide_branch else 2)]
                            for k, l in terms:
                                at = slice(m * P, (m + 1) * P)
                                if wide_branch:
                                    lhs, rhs = w_gu_t32[:, w, k, at], n_t32[:, k, b * S:(b + 1) * S]
                                else:
                                    lhs, rhs = w_gu_t[:, w, k, at], n_t16[:, l, k, b * S:(b + 1) * S]
                                ins = pe.matmul(dst, lhs, rhs, start=(k, l) == terms[0], stop=(k, l) == terms[-1])
                        ins.then_inc(hid_filled, 1)
                    elif kind == "down":
                        _, b, m = step
                        n = b * MT + m
                        if wide_branch:
                            pe.wait_ge(h_made, n + 1)
                        else:
                            pe.wait_ge(h_high, n + 1)
                            pe.wait_ge(h_low, n + 1)
                        if m == 0 and b >= 1:
                            pe.wait_ge(y_read, 2 * b)
                        for t in range(QT):
                            dst = ps[:, Y_BANKS[t // 2], (t % 2) * D:(t % 2 + 1) * D]
                            rows = slice(t * P, (t + 1) * P)
                            for l in range(1 if wide_branch else 2):
                                if wide_branch:
                                    lhs, rhs = h32[:, n % NHB, rows], w_d_t32[:, m, :]
                                else:
                                    lhs, rhs = h16[:, n % NHB, l, rows], w_d_t[:, m, :]
                                ins = pe.matmul(dst, lhs, rhs, start=(m == 0 and t % 2 == 0 and l == 0),
                                                stop=(m == MT - 1), skip_group_check=True)
                        ins.then_inc(h_used, 1)

            pe.wait_ge(w_flag_ready, 1)
            wide_w = pe.value_load(w_flag[0:1, 0:1], min_val=0, max_val=1 << 20)
            with pe.If(wide_w > 0):
                ffn_pe(True)
            with pe.Else():
                ffn_pe(False)


_INS = ['x', 'ctx_2048', 'mask_BxS2_ik0', 'g_xattn', 'g_ffn', 'L0_xattn_b', 'L0_ffn_w_gate', 'L0_ffn_w_up',
        'L0_ffn_w_down']
_OUTS = [((4, 512, 256), 'float32')]


def kernel(**inputs):
    import numpy as _np
    import concourse.bacc as _bacc
    from concourse import mybir as _mybir
    from concourse.bass_utils import run_bass_kernel_spmd as _run

    nc = _bacc.Bacc("TRN2", target_bir_lowering=False, num_devices=1)
    arrays, args = {}, []
    for name in _INS:
        a = _np.ascontiguousarray(inputs[name])
        arrays[f"in_{name}_dram"] = a
        args.append(nc.dram_tensor(f"in_{name}_dram", a.shape, _mybir.dt.from_np(a.dtype), kind="ExternalInput").ap())
    for i, (shape, dtype) in enumerate(_OUTS):
        dt = _mybir.dt.from_np(_np.dtype(dtype))
        args.append(nc.dram_tensor(f"out_{i}_dram", shape, dt, kind="ExternalOutput").ap())
    flamingo_block_kernel(nc, *args)
    r = _run(nc, [arrays], core_ids=[0])
    got = tuple(r.results[0][f"out_{i}_dram"] for i in range(len(_OUTS)))
    return got[0]
```

```python
from contextlib import ExitStack

import concourse.bass as bass
from concourse import mybir

F32 = mybir.dt.float32
F16 = mybir.dt.float16
BF16 = mybir.dt.bfloat16
I32 = mybir.dt.int32
ALU = mybir.AluOpType
ACT = mybir.ActivationFunctionType
AX = mybir.AxisListType

P = 128
NH, DH = 8, 32
HG = P // DH
NG = NH // HG
NPART = 3
LN_EPS = 1e-5
MASK_STEP = -1e30
W_SCALE = 1.0 / 127.0
W_LIMIT = 2047.0
H_SHRINK = 1.0 / 8.0
SQUARES = 512
WARM_UP = 8
K_LIMIT = 60000.0



WIDE = "wide_"


class Plan:

    def __init__(self, common, branch, early_banks, banks, emptied_by):
        self.emptied_by = emptied_by
        self.nth, self.of_kind, self.fill, self.who, self.rank = {}, {}, {}, [], []
        self.banks, self.before, last = [], [], {}
        for place, step in enumerate(common + branch):
            kind = step[0].removeprefix(WIDE)
            assert step not in self.nth, step
            self.nth[step] = len(self.of_kind.setdefault(kind, []))
            self.of_kind[kind].append(step)
            engine = emptied_by_engine(kind, step)
            if engine is not None:
                n = self.fill[step] = len(self.who)
                choice = early_banks if place < len(common) else banks
                bank = choice[n % len(choice)]
                self.banks.append(bank)
                self.before.append(last.get(bank))
                last[bank] = n
                self.who.append(engine)
                self.rank.append(self.who.count(engine))

    def bank(self, step):
        return self.banks[self.fill[step]]

    def filled(self, step):
        return self.fill[step] + 1

    def emptied(self, step):
        n = self.fill[step]
        return self.emptied_by[self.who[n]], self.rank[n]

    def last_user(self, step):
        n = self.before[self.fill[step]]
        return None if n is None else (self.emptied_by[self.who[n]], self.rank[n])

    def early_users(self, bank):
        mine = [n for n, b in enumerate(self.banks) if b == bank]
        return [(self.emptied_by[who], max(self.rank[n] for n in mine if self.who[n] == who))
                for who in self.emptied_by if any(self.who[n] == who for n in mine)]


def emptied_by_engine(kind, step):
    if kind in ("mask_t", "k_stack", "flag_sum", "row_max", "attn_t", "k_block"):
        return "dve"
    if kind in ("mask_rows", "max_t", "q_wide", "n_t"):
        return "act"
    if kind == "q_stack":
        return "dve" if step[1:] == (1, 1) else "act"
    if kind == "w_t":
        return "dve"
    if kind == "w_wide":
        return "act" if step[1] % 2 else "dve"
    return None


def norm1_on_pool(step):
    return step[0] == "norm1" and step[1] in (2, 3)


def narrow_steps(B, MT, NC):
    c, R = NC - 1, 2 * B
    queries = lambda h: [("q_stack", h // 2, 2 * (h % 2) + i) for i in range(2)]
    maxima = lambda h: [("row_max", h // 2, c, 2 * (h % 2) + i, g) for i in range(2) for g in range(NG)]
    sq = lambda i: ("squares", i)
    steps = [("stats", 1, 0), ("mask_t",), ("warm_up",), ("norm1", 0), ("high", 1, 0), ("low", 1, 0), ("k_parts", 0),
             ("mask_parts",), ("mask_rows",), ("dup", 0), ("stats", 1, 1), ("q_stack", 0, 0), ("k_stack", 0),
             ("norm1", 1), ("q_stack", 0, 1), ("high", 1, 1), ("low", 1, 1), *maxima(0)[:3], ("dup", 1),
             *maxima(0)[3:], sq(0), ("q_stack", 0, 2), ("max_split", 0), ("max_t", 0), ("q_stack", 0, 3),
             ("k_parts", 1), ("stats", 1, 2)]
    chores = [[sq(1)], [("w_cast", 0)], [sq(2), sq(3)], [("k_stack", 1)], [("w_t", 0), sq(4)],
              [("w_cast", 1), ("w_t", 1), sq(5)],
              [sq(6), sq(9)], [("w_t", 2)], [sq(7), ("w_t", 3)], [sq(8), ("check",)], [("flag_sum",)], [("w_cast", 2)],
              [("w_t", 4)], [("w_t", 5)], [], [("k_parts", 2)], [("k_stack", 2)]]
    units = [(h, m) for h in range(R) for m in range(MT)]
    LAG = 3

    def put(*what, when=True):
        steps.extend(what if when else ())

    downs = [0]

    def unit(n, lag=LAG):
        put(("hidden", *units[n % len(units)]), when=0 <= n < len(units))
        put(("h_split", *units[(n - 1) % len(units)]), when=0 <= n - 1 < len(units))
        for d in range(downs[0], min(n - lag + 1, len(units))):
            put(("down", *units[d]))
            put(("finish", d // MT), when=d % MT == MT - 1)
        downs[0] = max(downs[0], n - lag + 1)

    def product(n):
        put(("product", *units[n % len(units)]), when=0 <= n < len(units))

    for r in range(R):
        n = (r - 3) * MT + MT // 2
        ahead, queued, done, normed = r + 1 < R, r + 2 < R, r >= 1, r >= 2
        mx = maxima(r + 1) if ahead else [None] * 4
        q = queries(r + 2) if queued else [None] * 2
        b, half = divmod(r, 2)
        pb, ph = divmod(r - 1, 2)

        def scores(i):
            put(("scores", b, half, i // 2, c, i % 2))

        def chore():
            put(*(chores.pop(0) if chores else ()))

        scores(0)
        put(("norm2", r - 2), when=normed)
        unit(n)
        chore()
        put(mx[0], when=ahead)
        product(n)
        put(("weigh_o", pb, ph, 1, c), ("weigh_d", pb, ph, 0, c), ("weigh_d", pb, ph, 1, c),
            ("o_copy", pb, ph, 1), when=done)
        put(("high", 2, r - 2), ("low", 2, r - 2), when=normed)
        put(("norm1", r + 2), ("high", 1, r + 2), when=queued)
        put(mx[1], when=ahead)
        unit(n + 1)
        chore()
        scores(1)
        put(mx[2], when=ahead)
        product(n + 1)
        put(("low", 1, r + 2), when=queued)
        unit(n + 2)
        chore()
        put(mx[3], when=ahead)
        put(("n_t", r - 2), when=normed)
        put(("max_split", r + 1), when=ahead)
        scores(2)
        put(("attn_t", pb, 2 * ph), when=done)
        product(n + 2)
        put(("dup", r + 2), when=queued)
        put(("weigh_o", b, half, 0, c))
        unit(n + 3)
        chore()
        put(("attn_t", pb, 2 * ph + 1), when=done)
        put(("o_copy", b, half, 0))
        product(n + 3)
        unit(n + 4)
        chore()
        put(("max_t", r + 1), when=ahead)
        put(q[0], when=queued)
        product(n + 4)
        scores(3)
        chore()
        put(("stats", 2, r - 1), when=done)
        unit(n + 5)
        put(q[1], when=queued)
        product(n + 5)
        put(("k_parts", b + 2), when=r % 2 == 1 and r > 1 and b + 2 < B)
        put(("k_stack", b + 1), when=r % 2 == 0 and r > 2 and b + 1 < B)
        put(("stats", 1, r + 3), when=r + 3 < R)
        if r == 1:
            split = len(steps)

    h, b, n = R - 1, B - 1, (R - 3) * MT + MT // 2
    put(("norm2", h - 1))
    unit(n)
    product(n)
    put(("weigh_o", b, 1, 1, c), ("weigh_d", b, 1, 0, c), ("weigh_d", b, 1, 1, c), ("o_copy", b, 1, 1))
    put(("high", 2, h - 1), ("low", 2, h - 1))
    unit(n + 1)
    put(("attn_t", b, 2), ("attn_t", b, 3))
    product(n + 1)
    put(("n_t", h - 1))
    unit(n + 2)
    product(n + 2)
    unit(n + 3)
    put(("stats", 2, h))
    put(("norm2", h))
    product(n + 3)
    unit(n + 4)
    put(("high", 2, h), ("low", 2, h))
    product(n + 4)
    unit(n + 5)
    product(n + 5)
    for i in range(6, len(units) - n + 1):
        if i == 8:
            put(("n_t", h))
        unit(n + i, LAG if i < 9 else LAG + 2)
        product(n + i)
    for n in range(len(units) + 1, len(units) + LAG + 2):
        unit(n, LAG + 2)
    return steps[:split], steps[split:]


def wide_steps(B, MT, NC):
    R, c = 2 * B, NC - 1
    drain = [("weigh_o", 0, 1, 1, c), ("weigh_d", 0, 1, 0, c), ("weigh_d", 0, 1, 1, c), ("o_copy", 0, 1, 1)]
    steps = []
    for b in range(B):
        steps += [("load", b)] + [(part, *w, 2 * b + h) for h in range(2) for part, w in (("stats", (1,)), ("norm1", ()))]
        steps += [("q_wide", b, g) for g in range(NG)] + [("mask_rows", b)]
        steps += [("k_block", b, c, g) for c in range(NC) for g in range(NG)]
        steps += [("row_max", b, c, qt, g) for c in range(NC) for qt in range(4) for g in range(NG)]
        steps += [(kind, 2 * b + half) for half in range(2) for kind in ("max_split", "max_t")]
        for half in range(2):
            for g in range(NG):
                for c in range(NC):
                    steps += [("scores", b, half, g, c, 0), ("scores", b, half, g, c, 1),
                              ("weigh_o", b, half, g, c), ("weigh_d", b, half, g, c)]
                steps.append(("o_copy", b, half, g))
            steps += [("attn_t", b, 2 * half), ("attn_t", b, 2 * half + 1)]
    steps += [("w_wide", i) for i in range(12)]
    for r in range(R):
        steps += [("stats", 2, r), ("norm2", r), ("n_t", r)]
        steps += [(kind, r, m) for m in range(MT) for kind in ("hidden", "product")]
        steps += [("down", r, m) for m in range(MT)] + [("finish", r)]
    return drain, [(WIDE + s[0], *s[1:]) for s in steps]


def flamingo_block_kernel(nc, x, ctx, mask, g_xattn, g_ffn, attn_b, w_gate, w_up, w_down, out):
    B, S, D = x.shape
    SK = ctx.shape[1]
    HID = w_gate.shape[0]
    QT, NC, MT, KD = S // P, SK // P, HID // P, D // P
    LAST = NC - 1
    NT, R, SH = B * QT, 2 * B, S // 2
    assert (NH * DH, ctx.shape[2], D, QT, NC) == (D, 2 * D, 256, 4, 4)
    Q_SCALE_SQ = 1.0 / DH

    stack = ExitStack()
    with stack:
        def sb(name, shape, dt):
            return stack.enter_context(nc.sbuf_tensor(name, shape, dt))

        def sem(name):
            return stack.enter_context(nc.semaphore(name))

        x_sb = sb("x_sb", [P, NT, D], F32)
        kv = sb("kv", [P, B, 2 * D], F32)
        kv_rest = sb("kv_rest", [P, LAST, 2 * D], F32)
        NLB = 4
        norm32 = sb("norm32", [P, NLB, 2, D], F32)
        norm16 = sb("norm16", [P, 2, 2, 2, D], F16)
        q_parts = sb("q_parts", [P, NLB, 2 * NH, 2, 2, DH], F16)
        k_parts = sb("k_parts", [P, 2, NH, 2, 2, DH], F16)
        q_stacks = sb("q_stacks", [P, B, NH, S], F16)
        k_stacks = sb("k_stacks", [P, B, NH, P], F16)
        NPB = 8
        probs = sb("probs", [P, NPB, 2 * SH], F32)
        o_sb = sb("o_sb", [P, 2, NG + 1, SH], F32)
        w_raw = sb("w_raw", [P, 3, MT * D], I32)
        w16 = sb("w16", [P, 3, MT * D], F16)
        w_gu_t = sb("w_gu_t", [P, 2, KD, HID], F16)
        w_d_t = sb("w_d_t", [P, MT, D], F16)
        n_t16 = sb("n_t16", [P, 2, 2 * KD, SH], F16)
        NHB = 4
        tanh_h = sb("tanh_h", [P, 2, SH], F32)
        gated = sb("gated", [P, 2, SH], F32)
        h32 = sb("h32", [P, NHB, SH], F32)
        h16 = sb("h16", [P, 2, MT, 2, SH], F16)
        attn = sb("attn", [P, 2, D], F32)
        ident32 = sb("ident32", [P, P], F32)
        ident16 = sb("ident16", [P, P], F16)
        identb = sb("identb", [P, P], BF16)
        ones32 = sb("ones32", [P, 1], F32)
        sum_cols = sb("sum_cols", [P, NG, DH], F32)
        head_rows = sb("head_rows", [P, NH], BF16)
        max_sel = sb("max_sel", [P, NH, P], BF16)
        ones_b = sb("ones_b", [P, P], BF16)
        neg_half = sb("neg_half", [P, 2], F32)
        gates = sb("gates", [P, 3], F32)
        tanh_g = sb("tanh_g", [P, 2], F32)
        y_scale = sb("y_scale", [P, 1], F32)
        stats = sb("stats", [P, 2, 6], F32)
        mv = sb("mv", [P, NLB, 2, 2], F32)
        var_eps = sb("var_eps", [P, NLB, 2], F32)
        rstd = sb("rstd", [P, NLB, 2], F32)
        neg_mean = sb("neg_mean", [P, NLB, 2], F32)
        mask_raw = sb("mask_raw", [B * NC, P], I32)
        mask_f = sb("mask_f", [B * NC, P], F32)
        mask_k = sb("mask_k", [P, B * NC], F32)
        key_bias = sb("key_bias", [P, B * NC], F32)
        rest = sb("rest", [P, B * NC], F32)
        bias_parts = sb("bias_parts", [P, B * NC, NPART], BF16)
        bias_rows = sb("bias_rows", [P, B * NC, P], BF16)
        NSUMS = 3 * MT * D // SQUARES + 1
        square_sums = sb("square_sums", [P, NSUMS], F32)
        dump = sb("dump", [P, B, D], F32)
        NZERO = B * NC + NSUMS
        checks = sb("checks", [P, NZERO + B], F32)
        verdict = sb("verdict", [1, 4], F32)
        wide_flag = sb("wide_flag", [1, 1], I32)
        max_c = sb("max_c", [P, QT, NH, NC], F32)
        neg_max = sb("neg_max", [P, QT, NH], F32)
        max_rest = sb("max_rest", [P, QT, NH], F32)
        max_cols = sb("max_cols", [P, QT, P], BF16)
        max_rows = sb("max_rows", [P, 2, SH], BF16)
        recip = sb("recip", [P, 2, NH], F32)
        max_parts = max_cols[:, :, 0:NPART * NH].rearrange("p t (a h) -> p t a h", a=NPART)
        q_mem = q_stacks[:, :, :, :].rearrange("p b h s -> p (b h s)").bitcast(F32)
        k_blocks = q_mem[:, 0:NC * NH * P].rearrange("p (c h k) -> p c h k", c=NC, h=NH)
        q_wide = q_mem[:, NC * NH * P:NC * NH * P + NG * S].rearrange("p (g s) -> p g s", g=NG)
        w_gu_t32 = q_mem[:, 0:2 * KD * HID].rearrange("p (w k h) -> p w k h", w=2, k=KD)
        w_d_t32 = q_mem[:, 2 * KD * HID:2 * KD * HID + MT * D].rearrange("p (m d) -> p m d", m=MT)
        w32 = q_mem[:, 2 * KD * HID + MT * D:2 * KD * HID + 2 * MT * D]
        n_t32 = n_t16[:, :, :, :].rearrange("p n k s -> p (n k s)").bitcast(F32).rearrange(
            "p (n k s) -> p n k s", n=2, k=KD)
        h_wide = h16[:, :, :, :, :].rearrange("p n m l s -> p (n m l s)").bitcast(F32).rearrange(
            "p (n m s) -> p n m s", n=2, m=MT)

        ps = stack.enter_context(nc.psum_tensor("ps", [P, 8, 512], F32))
        WORK, SCORES, O_BANK, HID_BANKS, Y_BANK = (0, 1), (2, 3), 4, (5, 6), 7

        def bank32(n):
            return ps[:, n, :]

        def bank16(n):
            return ps[:, n, :].bitcast(F16)

        def bankb(n):
            return ps[:, n, :].bitcast(BF16)

        def sums_at(wide):
            return bank32(HID_BANKS[0])[:, 0:SH] if wide else bank32(O_BANK)[:, SH:2 * SH]

        x_loaded = [sem(f"x_loaded{r}") for r in range(R)]
        kv_loaded = [sem(f"kv_loaded{b}") for b in range(B)]
        kv_rest_loaded = sem("kv_rest_loaded")
        mask_loaded, gates_loaded = sem("mask_loaded"), sem("gates_loaded")
        w_loaded = [sem(f"w_loaded{i}") for i in range(3)]
        pool_done = sem("pool_done")
        CONSTS = 12 + NPART
        selector_ready = sem("selector_ready")
        zeros_written = sem("zeros_written")
        tanh_ready = sem("tanh_ready")
        dve_done = sem("dve_done")
        mask_cast, bias_split = sem("mask_cast"), sem("bias_split")
        key_bias_ready = sem("key_bias_ready")
        checks_made, squares_summed = sem("checks_made"), sem("squares_summed")
        flag_ready = sem("flag_ready")
        k_high, k_low = sem("k_high"), sem("k_low")
        var_ready, rstd_ready = sem("var_ready"), sem("rstd_ready")
        normed1, normed2 = sem("normed1"), sem("normed2")
        norm_high, norm_low, q_doubled = sem("norm_high"), sem("norm_low"), sem("q_doubled")
        w_cast, w_wide_cast = sem("w_cast"), sem("w_wide_cast")
        work_filled = sem("work_filled")
        emptied_by = {"dve": sem("work_emptied_dve"), "act": sem("work_emptied_act")}
        max_split = sem("max_split")
        scores_filled, exp_done = sem("scores_filled"), sem("exp_done")
        o_summed, weighed, o_copied = sem("o_summed"), sem("weighed"), sem("o_copied")
        x1_ready = sem("x1_ready")
        hid_filled, tanh_done, h_made = sem("hid_filled"), sem("tanh_done"), sem("h_made")
        h_high, h_low, down_done = sem("h_high"), sem("h_low"), sem("down_done")
        y_read = sem("y_read")
        stored = sem("stored")

        common, narrow = narrow_steps(B, MT, NC)
        drain, wide = wide_steps(B, MT, NC)
        plans = {is_wide: Plan(common, rest, WORK + HID_BANKS, WORK, emptied_by)
                 for is_wide, rest in ((False, narrow), (True, drain + wide))}
        branch = {False: narrow, True: drain + wide}

        def ln_slot(plan, kind, which, r):
            pre = WIDE if kind.startswith(WIDE) else ""
            return plan.nth[pre + "stats", which, r] % NLB

        def norm_before(plan, kind, which, r):
            pre = WIDE if kind.startswith(WIDE) else ""
            place = plan.nth[pre + "stats", which, r]
            return None if place < NLB else plan.of_kind["stats"][place - NLB]

        def wait_normed(eng, plan, stats_step):
            kind, which, r = stats_step
            step = (kind.replace("stats", f"norm{which}"), r)
            if step in plan.nth:
                eng.wait_ge(normed1 if which == 1 else normed2, plan.nth[step] + 1)

        def wait_norm_used(eng, plan, kind, which, r):
            before = norm_before(plan, kind, which, r)
            if before is None:
                return
            k, w, p = before
            if not k.startswith(WIDE):
                if ("low", w, p) in plan.nth:
                    eng.wait_ge(norm_low, plan.nth["low", w, p] + 1)
            elif w == 1:
                if (WIDE + "q_wide", p // 2, NG - 1) in plan.nth:
                    eng.wait_ge(work_filled, plan.filled((WIDE + "q_wide", p // 2, NG - 1)))
            else:
                eng.wait_ge(work_filled, plan.filled((WIDE + "n_t", p)))

        def norm_parts(plan, step):
            kind, which, r = step
            slot = ln_slot(plan, kind, which, r)
            if which == 2:
                n = r % 2
                return norm32[:, slot, :, :], norm16[:, n, 0, :, :], norm16[:, n, 1, :, :]
            full = norm32[:, slot, :, :].rearrange("p t (h d) -> p (t h) d", h=NH)
            return full, q_parts[:, r % NLB, :, 0, 0, :], q_parts[:, r % NLB, :, 0, 1, :]

        def key_parts(b):
            full = kv[:, b, 0:D].rearrange("p (h d) -> p h d", h=NH).unsqueeze(2).to_broadcast((P, NH, 2, DH))
            return full, k_parts[:, b % 2, :, 0, :, :], k_parts[:, b % 2, :, 1, :, :]

        def mask_blocks(step, table):
            blocks = table.rearrange("p (b c) k -> p b c k", c=NC)
            return blocks[:, :, LAST, :] if len(step) == 1 else blocks[:, step[1], :, :]

        def chunk_kv(b, c):
            return kv[:, b, :] if c == LAST else kv_rest[:, c, :]

        def q_stack_out(plan, step):
            _, b, qt = step
            return (q_stacks[:, b, :, qt * P:(qt + 1) * P],
                    bank16(plan.bank(step)).rearrange("p (h k) -> p h k", h=NH))

        def weights_out(plan, step):
            w, half = divmod(step[1], 2)
            got = bank16(plan.bank(step))[:, 0:MT * P].rearrange("p (m k) -> p m k", m=MT)
            if w < 2:
                return w_gu_t[:, w, half, :].rearrange("p (m k) -> p m k", m=MT), got
            return w_d_t[:, :, half * P:(half + 1) * P], got

        def wide_weights_out(plan, step):
            wh, part = divmod(step[1], 2)
            w, half = divmod(wh, 2)
            M2 = MT // 2
            got = bank32(plan.bank(step))[:, 0:M2 * P].rearrange("p (m k) -> p m k", m=M2)
            if w < 2:
                return (w_gu_t32[:, w, half, part * M2 * P:(part + 1) * M2 * P]
                        .rearrange("p (m k) -> p m k", m=M2), got)
            return w_d_t32[:, part * M2:(part + 1) * M2, half * P:(half + 1) * P], got

        block = stack.enter_context(nc.Block())

        def load_x(eng, r):
            eng.dma_start(x_sb[:, 2 * r:2 * r + 2, :],
                          x[r // 2, (r % 2) * SH:(r % 2 + 1) * SH, :].rearrange("(t p) d -> p t d", p=P)
                          ).then_inc(x_loaded[r], 16)

        def load_kv(eng, b):
            eng.dma_start(kv[:, b, :], ctx[b, LAST * P:SK, :]).then_inc(kv_loaded[b], 16)

        @block.sync
        def _(sp):
            load_x(sp, 0)
            for n, g in enumerate((g_xattn, g_ffn, attn_b)):
                sp.dma_start(gates[:, n:n + 1], g.partition_broadcast(P)).then_inc(gates_loaded, 16)
            load_x(sp, 1)
            load_kv(sp, 1)
            load_x(sp, 2)
            for i, w in ((0, w_gate), (1, w_up)):
                sp.dma_start(w_raw[:, i, :].rearrange("p (m d) -> p m d", d=D),
                             w.rearrange("(m p) d -> p m d", p=P)).then_inc(w_loaded[i], 16)
            load_x(sp, 3)
            sp.dma_start(w_raw[:, 2, :].rearrange("p (t h) -> p t h", h=HID),
                         w_down.rearrange("(t p) h -> p t h", p=P)).then_inc(w_loaded[2], 16)
            for b in range(2, B):
                load_kv(sp, b)
            for r in range(4, R):
                load_x(sp, r)

            def stores(is_wide):
                plan = plans[is_wide]
                for step in branch[is_wide]:
                    kind = step[0].removeprefix(WIDE)
                    if kind == "load":
                        b = step[1]
                        if b == 0:
                            sp.wait_ge(x1_ready, sum(s[0] == "attn_t" for s in common))
                            sp.wait_ge(var_ready, plan.nth["stats", 2, 0] + 1)
                            load_x(sp, 0)
                        if b >= 1:
                            used = plan.nth[WIDE + "weigh_d", b - 1, 1, NG - 1, NC - 1]
                            sp.wait_ge(weighed, used + 1)
                        sp.dma_start(kv_rest[:, :, :], ctx[b, 0:LAST * P, :].rearrange("(c p) d -> p c d", p=P)
                                     ).then_inc(kv_rest_loaded, 16)
                    elif kind == "finish":
                        r = step[1]
                        sp.wait_ge(y_read, r + 1)
                        sp.dma_start(out[r // 2, (r % 2) * SH:(r % 2 + 1) * SH, :].rearrange("(t p) d -> p t d", p=P),
                                     x_sb[:, 2 * r:2 * r + 2, :]).then_inc(stored, 16)

            sp.wait_ge(flag_ready, 1)
            flag = sp.value_load(wide_flag[0:1, 0:1], min_val=0, max_val=2)
            with sp.If(flag > 0):
                stores(True)
            with sp.Else():
                stores(False)
            sp.wait_ge(stored, 16 * R)

        @block.gpsimd
        def _(pool):
            for m in (ident32[:, :], ident16[:, :], identb[:, :], sum_cols[:, :, :]):
                pool.memset(m, 0.0).then_inc(pool_done, 1)
            pool.memset(neg_half[:, :], -0.5).then_inc(pool_done, 1)
            pool.memset(ones32[:, :], 1.0).then_inc(pool_done, 1)
            pool.memset(ones_b[:, :], 1.0).then_inc(pool_done, 1)
            pool.memset(head_rows[:, :], 0.0).then_inc(pool_done, 1)
            pool.wait_ge(pool_done, 8)
            for m in (ident32, ident16, identb):
                pool.affine_select(out=m[:, :], in_=m[:, :], compare_op=ALU.not_equal, fill=1.0, base=0,
                                   pattern=[[-1, P]], channel_multiplier=1).then_inc(pool_done, 1)
            pool.affine_select(out=sum_cols[:, :, :], in_=sum_cols[:, :, :], compare_op=ALU.not_equal, fill=1.0,
                               base=0, pattern=[[-1, NG], [1, DH]], channel_multiplier=0).then_inc(pool_done, 1)
            for part in range(NPART):
                if part:
                    pool.wait_ge(pool_done, 12 + part)
                pool.affine_select(out=head_rows[:, :], in_=head_rows[:, :], compare_op=ALU.not_equal, fill=1.0,
                                   base=-NH * part, pattern=[[-1, NH]], channel_multiplier=1).then_inc(pool_done, 1)

            def run(plan, steps):
                for step in steps:
                    kind = step[0].removeprefix(WIDE)
                    if kind == "stats":
                        place = plan.nth[step]
                        pool.wait_ge(var_ready, place + 1)
                        pool.tensor_tensor(rstd[:, place % NLB, :], var_eps[:, place % NLB, :], neg_half[:, :],
                                           ALU.pow).then_inc(rstd_ready, 1)
                    elif kind == "norm1" and norm1_on_pool(step):
                        r = step[1]
                        slot = ln_slot(plan, step[0], 1, r)
                        pool.wait_ge(rstd_ready, plan.nth[step[0].replace("norm1", "stats"), 1, r] + 1)
                        wait_norm_used(pool, plan, step[0], 1, r)
                        pool.wait_ge(normed1, plan.nth[step])
                        for i in range(2):
                            ins = pool.tensor_scalar(norm32[:, slot, i, :], x_sb[:, 2 * r + i, :],
                                                     neg_mean[:, slot, i:i + 1], rstd[:, slot, i:i + 1],
                                                     ALU.add, ALU.mult)
                        ins.then_inc(normed1, 1)
                    elif kind == "norm2":
                        r = step[1]
                        slot = ln_slot(plan, step[0], 2, r)
                        pre = step[0].replace("norm2", "stats")
                        pool.wait_ge(rstd_ready, plan.nth[pre, 2, r] + 1)
                        wait_norm_used(pool, plan, step[0], 2, r)
                        for i in range(2):
                            ins = pool.tensor_scalar(norm32[:, slot, i, :], x_sb[:, 2 * r + i, :],
                                                     neg_mean[:, slot, i:i + 1], rstd[:, slot, i:i + 1],
                                                     ALU.add, ALU.mult)
                        ins.then_inc(normed2, 1)
                    elif kind == "low":
                        pool.wait_ge(norm_high, plan.nth["high", step[1], step[2]] + 1)
                        full, high, low = norm_parts(plan, step)
                        pool.tensor_tensor(low, full, high, ALU.subtract).then_inc(norm_low, 1)
                    elif kind == "k_parts":
                        b = step[1]
                        pool.wait_ge(k_high, b + 1)
                        full, high, low = key_parts(b)
                        pool.tensor_tensor(low, full, high, ALU.subtract).then_inc(k_low, 1)
                    elif kind == "attn_t":
                        n = plan.nth[step]
                        t = step[1] * QT + step[2]
                        pool.wait_ge(*plan.emptied(step))
                        pool.tensor_tensor(x_sb[:, t, :], x_sb[:, t, :], attn[:, n % 2, :],
                                           ALU.add).then_inc(x1_ready, 1)
                    elif kind == "h_split":
                        _, r, m = step
                        n = r * MT + m
                        pool.wait_ge(h_high, n + 1)
                        pool.tensor_tensor(h16[:, r % 2, m, 1, :], h32[:, n % NHB, :], h16[:, r % 2, m, 0, :],
                                           ALU.subtract).then_inc(h_low, 1)

            run(plans[False], common)
            pool.wait_ge(flag_ready, 1)
            flag = pool.value_load(wide_flag[0:1, 0:1], min_val=0, max_val=2)
            with pool.If(flag > 0):
                run(plans[True], branch[True])
            with pool.Else():
                run(plans[False], narrow)

        @block.scalar
        def _(act):
            act.dma_start(mask_raw[:, :], mask.rearrange("b (c k) -> (b c) k", k=P)).then_inc(mask_loaded, 16)
            load_kv(act, 0)
            act.wait_ge(pool_done, CONSTS)
            act.activation(max_sel[:, :, :], head_rows[:, :].unsqueeze(2).to_broadcast((P, NH, P)), ACT.Copy
                           ).then_inc(selector_ready, 1)

            def run(plan, steps):
                for step in steps:
                    kind, is_wide = step[0].removeprefix(WIDE), step[0].startswith(WIDE)
                    if kind == "high":
                        _, which, r = step
                        wait_normed(act, plan, ("stats", which, r))
                        old = r - (NLB if which == 1 else 2)
                        if old >= 0:
                            act.wait_ge(work_filled, plan.filled(
                                ("q_stack", old // 2, 2 * (old % 2) + 1) if which == 1 else ("n_t", old)))
                        full, high, _ = norm_parts(plan, step)
                        act.activation(high, full, ACT.Copy).then_inc(norm_high, 1)
                        if step == ("high", 1, 1):
                            act.wait_ge(gates_loaded, 48)
                            act.activation(tanh_g[:, :], gates[:, 0:2], ACT.Tanh).then_inc(tanh_ready, 1)
                    elif kind == "mask_rows":
                        act.wait_ge(zeros_written, 1)
                        act.wait_ge(work_filled, plan.filled(step))
                        act.activation(mask_blocks(step, bias_rows)[0:NPART, :, :],
                                       bankb(plan.bank(step))[0:NPART, 0:4 * P].rearrange("p (c k) -> p c k", k=P),
                                       ACT.Copy).then_inc(emptied_by["act"], 1)
                    elif kind == "q_stack" and emptied_by_engine(kind, step) == "act":
                        act.wait_ge(work_filled, plan.filled(step))
                        act.activation(*q_stack_out(plan, step), ACT.Copy).then_inc(emptied_by["act"], 1)
                    elif kind == "w_wide" and emptied_by_engine(kind, step) == "act":
                        act.wait_ge(work_filled, plan.filled(step))
                        dst, src = wide_weights_out(plan, step)
                        act.activation(dst, src, ACT.Copy).then_inc(emptied_by["act"], 1)
                    elif kind == "squares":
                        i, n = step[1], plan.nth[step]
                        if n:
                            act.wait_ge(squares_summed, n)
                        if i < NSUMS - 1:
                            w, part = divmod(i, MT * D // SQUARES)
                            act.wait_ge(w_loaded[w], 16)
                            act.activation(dump[:, 0:SQUARES // D, :],
                                           w_raw[:, w, part * SQUARES:(part + 1) * SQUARES].rearrange(
                                               "p (m d) -> p m d", d=D), ACT.Square,
                                           accum_out=square_sums[:, i:i + 1]).then_inc(squares_summed, 1)
                        else:
                            for b in range(B):
                                act.wait_ge(kv_loaded[b], 16)
                            act.activation(dump[:, :, :], kv[:, :, 0:D], ACT.Square, scale=W_LIMIT / K_LIMIT,
                                           accum_out=square_sums[:, i:i + 1]).then_inc(squares_summed, 1)
                    elif kind == "q_wide":
                        act.wait_ge(work_filled, plan.filled(step))
                        act.activation(q_wide[:, step[2], :], bank32(plan.bank(step)),
                                       ACT.Copy).then_inc(emptied_by["act"], 1)
                    elif kind == "max_t":
                        n = plan.nth[step]
                        act.wait_ge(work_filled, plan.filled(step))
                        act.activation(max_rows[:, n % 2, :], bankb(plan.bank(step))[:, 0:SH],
                                       ACT.Copy).then_inc(emptied_by["act"], 1)
                    elif kind == "scores":
                        b, c, j = step[1], step[4], plan.nth[step]
                        act.wait_ge(scores_filled, j + 1)
                        act.wait_ge(key_bias_ready, 1)
                        if j >= NPB:
                            act.wait_ge(weighed, (j - NPB) // 2 + 1)
                        n = b * NC + c
                        act.activation(probs[:, j % NPB, :], bank32(SCORES[j % 2]), ACT.Exp,
                                       bias=key_bias[:, n:n + 1]).then_inc(exp_done, 1)
                    elif kind == "o_copy":
                        _, b, half, g = step
                        n = plan.nth[step]
                        act.wait_ge(o_summed, n + 1)
                        if n >= 2 * NG and g == 0:
                            pb, ph = plan.of_kind["o_copy"][n - 2 * NG][1:3]
                            pre = plan.of_kind["o_copy"][n - 2 * NG][0].replace("o_copy", "attn_t")
                            if (pre, pb, 2 * ph + 1) in plan.nth:
                                act.wait_ge(work_filled, plan.filled((pre, pb, 2 * ph + 1)))
                        buf = (n // NG) % 2
                        if g < NG - 1:
                            act.activation(o_sb[:, buf, g, :], bank32(O_BANK)[:, 0:SH], ACT.Copy
                                           ).then_inc(o_copied, 1)
                        else:
                            last = (step[0].replace("o_copy", "weigh_d"), b, half, g, LAST)
                            act.wait_ge(weighed, plan.nth[last] + 1)
                            if is_wide:
                                act.activation(o_sb[:, buf, NG, :], sums_at(True), ACT.Copy)
                                act.activation(o_sb[:, buf, g, :], bank32(O_BANK)[:, 0:SH], ACT.Copy
                                               ).then_inc(o_copied, 1)
                            else:
                                act.activation(o_sb[:, buf, g:g + 2, :],
                                               bank32(O_BANK).rearrange("p (g s) -> p g s", g=2), ACT.Copy
                                               ).then_inc(o_copied, 1)
                    elif kind == "n_t":
                        r = step[1]
                        act.wait_ge(work_filled, plan.filled(step))
                        if r >= 2:
                            act.wait_ge(hid_filled, (r - 1) * MT)
                        if is_wide:
                            act.activation(n_t32[:, r % 2, :, :].rearrange("p k (t s) -> p k t s", t=2),
                                            bank32(plan.bank(step)).rearrange("p (k t s) -> p k t s", k=KD, t=2),
                                           ACT.Copy).then_inc(emptied_by["act"], 1)
                        else:
                            act.activation(n_t16[:, r % 2, :, :].rearrange("p k (t s) -> p k t s", t=2),
                                            bank16(plan.bank(step)).rearrange("p (k t s) -> p k t s", k=2 * KD, t=2),
                                           ACT.Copy).then_inc(emptied_by["act"], 1)
                    elif kind == "hidden":
                        n = step[1] * MT + step[2]
                        act.wait_ge(hid_filled, n + 1)
                        if n >= 2:
                            act.wait_ge(h_made, n - 1)
                        act.activation(tanh_h[:, n % 2, :], bank32(HID_BANKS[n % 2])[:, 0:SH], ACT.Tanh,
                                       scale=0.5 * W_SCALE).then_inc(tanh_done, 1)
                    elif kind == "h_split":
                        _, r, m = step
                        n = r * MT + m
                        act.wait_ge(h_made, n + 1)
                        if r >= 2:
                            act.wait_ge(down_done, (r - 2) * MT + m + 1)
                        act.activation(h16[:, r % 2, m, 0, :], h32[:, n % NHB, :], ACT.Copy).then_inc(h_high, 1)

            run(plans[False], common)
            act.wait_ge(flag_ready, 1)
            flag = act.value_load(wide_flag[0:1, 0:1], min_val=0, max_val=2)
            with act.If(flag > 0):
                run(plans[True], branch[True])
            with act.Else():
                run(plans[False], narrow)

        @block.vector
        def _(dve):
            count = [0]

            def mine(ins):
                ins.then_inc(dve_done, 1)
                count[0] += 1

            def wait_mine():
                dve.wait_ge(dve_done, count[0])

            def mask_steps(step, plan):
                dve.wait_ge(mask_loaded, 16)
                dve.tensor_copy(mask_f[:, :], mask_raw[:, :]).then_inc(mask_cast, 1)
                dve.wait_ge(work_filled, plan.filled(step))
                dve.tensor_copy(mask_k[:, :], bank32(plan.bank(step))[:, 0:B * NC]).then_inc(emptied_by["dve"], 1)
                dve.wait_ge(*plan.emptied(step))
                mine(dve.tensor_scalar(key_bias[:, :], mask_k[:, :], -1.0, 1.0, ALU.mult, ALU.add))
                mine(dve.tensor_scalar(checks[:, 0:B * NC], mask_k[:, :], 0.0, None, ALU.not_equal))
                last = mask_k[:, :].rearrange("p (b c) -> p b c", c=NC)[:, :, LAST]
                mine(dve.tensor_scalar(checks[:, NZERO:NZERO + B], last, 1.0, None, ALU.is_ge))
                wait_mine()
                mine(dve.memset(checks[:, 0:B * NC].rearrange("p (b c) -> p b c", c=NC)[:, :, LAST], 0.0))

            def mask_parts_steps():
                wait_mine()
                dve.wait_ge(gates_loaded, 48)
                mine(dve.tensor_scalar(key_bias[:, :], key_bias[:, :], MASK_STEP, gates[:, 2:3], ALU.mult, ALU.add))
                wait_mine()
                dve.tensor_scalar(key_bias[:, :], key_bias[:, :], 3e38, -3e38, ALU.min, ALU.max
                                  ).then_inc(key_bias_ready, 1)
                dve.wait_ge(key_bias_ready, 1)
                mine(dve.tensor_copy(bias_parts[:, :, 0], key_bias[:, :]))
                wait_mine()
                mine(dve.tensor_tensor(rest[:, :], key_bias[:, :], bias_parts[:, :, 0], ALU.subtract))
                wait_mine()
                mine(dve.tensor_copy(bias_parts[:, :, 1], rest[:, :]))
                wait_mine()
                dve.tensor_tensor(bias_parts[:, :, 2], rest[:, :], bias_parts[:, :, 1], ALU.subtract
                                  ).then_inc(bias_split, 1)

            def run(plan, steps):
                for step in steps:
                    kind, is_wide = step[0].removeprefix(WIDE), step[0].startswith(WIDE)
                    if kind == "stats":
                        _, which, r = step
                        place = plan.nth[step]
                        slot = place % NLB
                        if which == 1:
                            dve.wait_ge(x_loaded[r], 32 if is_wide and r == 0 else 16)
                        else:
                            attn_t = (step[0].replace("stats", "attn_t"), r // 2, 2 * (r % 2) + 1)
                            dve.wait_ge(x1_ready, plan.nth[attn_t] + 1)
                        before = norm_before(plan, *step)
                        if before is not None:
                            wait_normed(dve, plan, before)
                        for i in range(2):
                            mine(dve.bn_stats(stats[:, i, :], x_sb[:, 2 * r + i, :]))
                        wait_mine()
                        for i in range(2):
                            mine(dve.bn_aggr(mv[:, slot, i, :], stats[:, i, :]))
                        wait_mine()
                        if which == 2 or norm1_on_pool((step[0].replace("stats", "norm1"), r)):
                            dve.tensor_scalar(neg_mean[:, slot, :], mv[:, slot, :, 0], -1.0, None, ALU.mult)
                        dve.tensor_scalar(var_eps[:, slot, :], mv[:, slot, :, 1], LN_EPS,
                                          1.0 / Q_SCALE_SQ if which == 1 else 1.0, ALU.add, ALU.mult
                                          ).then_inc(var_ready, 1)
                    elif kind == "norm1" and not norm1_on_pool(step):
                        r = step[1]
                        slot = ln_slot(plan, step[0], 1, r)
                        dve.wait_ge(rstd_ready, plan.nth[step[0].replace("norm1", "stats"), 1, r] + 1)
                        wait_norm_used(dve, plan, step[0], 1, r)
                        if plan.nth[step]:
                            dve.wait_ge(normed1, plan.nth[step])
                        for i in range(2):
                            ins = dve.tensor_scalar(norm32[:, slot, i, :], x_sb[:, 2 * r + i, :],
                                                    mv[:, slot, i, 0:1], rstd[:, slot, i:i + 1],
                                                    ALU.subtract, ALU.mult)
                        ins.then_inc(normed1, 1)
                    elif kind == "dup":
                        r = step[1]
                        dve.wait_ge(norm_low, plan.nth["low", 1, r] + 1)
                        src, dst = (q_parts[:, r % NLB, :, a, :, :].rearrange("p h l d -> p h (l d)")
                                    for a in range(2))
                        dve.tensor_copy(dst, src).then_inc(q_doubled, 1)
                    elif kind == "mask_t":
                        mask_steps(step, plan)
                    elif kind == "mask_parts":
                        mask_parts_steps()
                    elif kind == "k_parts":
                        b = step[1]
                        dve.wait_ge(kv_loaded[b], 16)
                        full, high, _ = key_parts(b)
                        if b >= 2:
                            dve.wait_ge(work_filled, plan.filled(("k_stack", b - 2)))
                        dve.tensor_scalar(high, full, K_LIMIT, -K_LIMIT, ALU.min, ALU.max).then_inc(k_high, 1)
                    elif kind == "w_cast":
                        i = step[1]
                        dve.wait_ge(w_loaded[i], 16)
                        dve.tensor_scalar(w16[:, i, :], w_raw[:, i, :], W_LIMIT, -W_LIMIT, ALU.min, ALU.max
                                          ).then_inc(w_cast, 1)
                    elif kind == "check":
                        dve.wait_ge(squares_summed, NSUMS)
                        dve.tensor_scalar(checks[:, B * NC:NZERO], square_sums[:, :], W_LIMIT * W_LIMIT, None,
                                          ALU.is_gt).then_inc(checks_made, 1)
                    elif kind == "flag_sum":
                        dve.wait_ge(work_filled, plan.filled(step))
                        counts = bank32(plan.bank(step))
                        mine(dve.tensor_reduce(verdict[:, 0:1], counts[0:1, 0:NZERO], AX.X, ALU.add))
                        dve.tensor_reduce(verdict[:, 1:2], counts[0:1, NZERO:NZERO + B], AX.X, ALU.min
                                          ).then_inc(emptied_by["dve"], 1)
                        wait_mine()
                        dve.wait_ge(*plan.emptied(step))
                        mine(dve.scalar_tensor_tensor(out=verdict[:, 2:3], in0=verdict[:, 1:2], scalar=1.0,
                                                      in1=verdict[:, 0:1], op0=ALU.is_lt, op1=ALU.add))
                        wait_mine()
                        dve.tensor_scalar(wide_flag[:, :], verdict[:, 2:3], 1.0, None, ALU.min
                                          ).then_inc(flag_ready, 1)
                    elif kind == "q_stack" and emptied_by_engine(kind, step) == "dve":
                        dve.wait_ge(work_filled, plan.filled(step))
                        dve.tensor_copy(*q_stack_out(plan, step)).then_inc(emptied_by["dve"], 1)
                    elif kind == "k_stack":
                        dve.wait_ge(work_filled, plan.filled(step))
                        dve.tensor_copy(k_stacks[:, step[1], :, :],
                                        bank16(plan.bank(step)).rearrange("p (h k) -> p h k", h=NH)
                                        ).then_inc(emptied_by["dve"], 1)
                    elif kind in ("w_t", "w_wide"):
                        i = step[1]
                        if kind == "w_wide" and i % 4 == 0:
                            if i:
                                dve.wait_ge(work_filled, plan.filled((step[0], i - 1)))
                            dve.tensor_copy(w32, w_raw[:, i // 4, :]).then_inc(w_wide_cast, 1)
                        if emptied_by_engine(kind, step) == "dve":
                            dve.wait_ge(work_filled, plan.filled(step))
                            dst, src = weights_out(plan, step) if kind == "w_t" else wide_weights_out(plan, step)
                            dve.tensor_copy(dst, src).then_inc(emptied_by["dve"], 1)
                    elif kind == "k_block":
                        _, b, c, g = step
                        dve.wait_ge(work_filled, plan.filled(step))
                        for j in range(HG):
                            rows = slice(j * DH, (j + 1) * DH)
                            ins = dve.tensor_copy(k_blocks[rows, c, g * HG + j, :],
                                                  bank32(plan.bank(step))[rows, 0:P])
                        ins.then_inc(emptied_by["dve"], 1)
                    elif kind == "row_max":
                        _, b, c, qt, g = step
                        dve.wait_ge(work_filled, plan.filled(step))
                        n = plan.nth[step[0].replace("row_max", "max_split"), 2 * b + qt // 2]
                        if n >= 2 and qt % 2 == 0 and g == 0:
                            dve.wait_ge(max_split, n - 1)
                        if is_wide:
                            dst = max_c[:, qt, g * HG:(g + 1) * HG, c]
                        else:
                            dst = neg_max[:, qt, g * HG:(g + 1) * HG]
                        dve.tensor_reduce(dst, bank32(plan.bank(step)).rearrange("p (h k) -> p h k", h=HG),
                                          AX.X, ALU.max, negate=not is_wide).then_inc(emptied_by["dve"], 1)
                    elif kind == "max_split":
                        h, n = step[1], plan.nth[step]
                        b, qts = h // 2, slice(2 * (h % 2), 2 * (h % 2) + 2)
                        row_max = step[0].replace("max_split", "row_max")
                        dve.wait_ge(*plan.emptied((row_max, b, LAST, 2 * (h % 2) + 1, NG - 1)))
                        if n >= 2:
                            before = plan.of_kind["max_t"][n - 2]
                            dve.wait_ge(work_filled, plan.filled(before))
                        if n == 0:
                            dve.wait_ge(zeros_written, 1)
                        if is_wide:
                            mine(dve.tensor_reduce(neg_max[:, qts, :], max_c[:, qts, :, :], AX.X, ALU.max,
                                                   negate=True))
                            wait_mine()
                        mine(dve.tensor_copy(max_parts[:, qts, 0, :], neg_max[:, qts, :]))
                        wait_mine()
                        mine(dve.tensor_tensor(max_rest[:, qts, :], neg_max[:, qts, :], max_parts[:, qts, 0, :],
                                               ALU.subtract))
                        wait_mine()
                        mine(dve.tensor_copy(max_parts[:, qts, 1, :], max_rest[:, qts, :]))
                        wait_mine()
                        dve.tensor_tensor(max_parts[:, qts, 2, :], max_rest[:, qts, :], max_parts[:, qts, 1, :],
                                          ALU.subtract).then_inc(max_split, 1)
                    elif kind == "attn_t":
                        n = plan.nth[step]
                        got = bank32(plan.bank(step))
                        dve.wait_ge(work_filled, plan.filled(step))
                        if n == 0:
                            dve.wait_ge(tanh_ready, 1)
                        if n >= 2:
                            dve.wait_ge(x1_ready, n - 1)
                        sums = got[:, NG * P:(NG + 1) * P].rearrange("p (j d) -> p d j", d=DH)[:, 0:NG, :]
                        mine(dve.reciprocal(recip[:, n % 2, :].rearrange("p (g j) -> p g j", g=NG), sums))
                        wait_mine()
                        dve.scalar_tensor_tensor(
                            out=attn[:, n % 2, :].rearrange("p (h d) -> p h d", d=DH),
                            in0=got[:, 0:NG * P].rearrange("p (h d) -> p h d", d=DH), scalar=tanh_g[:, 0:1],
                            in1=recip[:, n % 2, :].unsqueeze(2).to_broadcast((P, NH, DH)),
                            op0=ALU.mult, op1=ALU.mult).then_inc(emptied_by["dve"], 1)
                    elif kind == "product":
                        _, r, m = step
                        n = r * MT + m
                        got = bank32(HID_BANKS[n % 2])
                        dve.wait_ge(tanh_done, n + 1)
                        mine(dve.scalar_tensor_tensor(out=gated[:, n % 2, :], in0=tanh_h[:, n % 2, :], scalar=1.0,
                                                      in1=got[:, 0:SH], op0=ALU.add, op1=ALU.mult))
                        wait_mine()
                        if is_wide:
                            dst = h_wide[:, r % 2, m, :]
                            if r >= 2:
                                dve.wait_ge(down_done, (r - 2) * MT + m + 1)
                        else:
                            dst = h32[:, n % NHB, :]
                            if n >= NHB:
                                dve.wait_ge(h_low, n - NHB + 1)
                        dve.scalar_tensor_tensor(out=dst, in0=got[:, SH:2 * SH],
                                                 scalar=0.5 * W_SCALE * W_SCALE * H_SHRINK, in1=gated[:, n % 2, :],
                                                 op0=ALU.mult, op1=ALU.mult).then_inc(h_made, 1)
                    elif kind == "finish":
                        r = step[1]
                        dve.wait_ge(down_done, MT * (r + 1))
                        rows = x_sb[:, 2 * r:2 * r + 2, :]
                        dve.scalar_tensor_tensor(out=rows, in0=bank32(Y_BANK).rearrange("p (t d) -> p t d", t=2),
                                                 scalar=y_scale[:, 0:1], in1=rows, op0=ALU.mult, op1=ALU.add
                                                 ).then_inc(y_read, 1)

            for m in (max_cols[:, :, :].rearrange("p t k -> p (t k)"),
                      bias_rows[:, :, :].rearrange("p c k -> p (c k)")):
                ins = dve.memset(m.bitcast(F32), 0.0)
            ins.then_inc(zeros_written, 1)
            run(plans[False], common)
            dve.wait_ge(tanh_ready, 1)
            mine(dve.tensor_scalar(y_scale[:, :], tanh_g[:, 1:2], W_SCALE / H_SHRINK, None, ALU.mult))
            wait_mine()
            dve.wait_ge(flag_ready, 1)
            flag = dve.value_load(wide_flag[0:1, 0:1], min_val=0, max_val=2)
            at_branch = count[0]
            with dve.If(flag > 0):
                run(plans[True], drain)
                for step in common:
                    if step[0] == "q_stack":
                        dve.wait_ge(*plans[True].emptied(step))
                dve.wait_ge(scores_filled, sum(s[0] == "scores" for s in common + drain))
                mine(dve.memset(k_blocks, 0.0))
                wait_mine()
                run(plans[True], wide)
            count[0] = at_branch
            with dve.Else():
                run(plans[False], narrow)

        @block.tensor
        def _(pe):
            pe.wait_ge(pool_done, CONSTS)

            def open_work(plan, step):
                last = plan.last_user(step)
                if last is not None:
                    pe.wait_ge(*last)
                return plan.bank(step)

            def run(plan, steps):
                for step in steps:
                    kind, is_wide = step[0].removeprefix(WIDE), step[0].startswith(WIDE)
                    of = lambda name: step[0].replace(kind, name)
                    if kind == "mask_t":
                        n = open_work(plan, step)
                        pe.wait_ge(mask_cast, 1)
                        pe.transpose(bank32(n)[:, 0:B * NC], mask_f[:, :], ident32[0:B * NC, 0:B * NC]
                                     ).then_inc(work_filled, 1)
                    elif kind == "warm_up":
                        for _ in range(WARM_UP):
                            pe.matmul(bank32(SCORES[0]), ones_b[:, :], ones_b[:, :].unsqueeze(1).to_broadcast((P, HG, P)),
                                      start=True, stop=True)
                    elif kind == "flag_sum":
                        n = open_work(plan, step)
                        pe.wait_ge(checks_made, 1)
                        pe.matmul(bank32(n)[0:1, 0:NZERO + B], ones32[:, 0:1], checks[:, :], start=True, stop=True
                                  ).then_inc(work_filled, 1)
                    elif kind == "mask_rows":
                        n = open_work(plan, step)
                        pe.wait_ge(bias_split, 1)
                        blocks = mask_blocks(step, bias_parts)
                        for i in range(4):
                            ins = pe.transpose(bankb(n)[0:NPART, i * P:(i + 1) * P], blocks[:, i, :], identb[:, :])
                        ins.then_inc(work_filled, 1)
                    elif kind == "q_stack":
                        _, b, qt = step
                        r, t = 2 * b + qt // 2, qt % 2
                        n = open_work(plan, step)
                        pe.wait_ge(q_doubled, r + 1)
                        for h in range(NH):
                            src = q_parts[:, r % NLB, t * NH + h, :, :, :].rearrange("p a l d -> p (a l d)")
                            ins = pe.transpose(bank16(n)[:, h * P:(h + 1) * P], src, ident16[:, :])
                        ins.then_inc(work_filled, 1)
                    elif kind == "k_stack":
                        b = step[1]
                        n = open_work(plan, step)
                        pe.wait_ge(k_high, b + 1)
                        pe.wait_ge(k_low, b + 1)
                        for h in range(NH):
                            src = k_parts[:, b % 2, h, :, :, :].rearrange("p l a d -> p (l a d)")
                            ins = pe.transpose(bank16(n)[:, h * P:(h + 1) * P], src, ident16[:, :])
                        ins.then_inc(work_filled, 1)
                    elif kind == "w_t":
                        w, half = divmod(step[1], 2)
                        n = open_work(plan, step)
                        pe.wait_ge(w_cast, w + 1)
                        for m in range(MT):
                            at = m * D + half * P if w < 2 else half * HID + m * P
                            ins = pe.transpose(bank16(n)[:, m * P:(m + 1) * P], w16[:, w, at:at + P], ident16[:, :])
                        ins.then_inc(work_filled, 1)
                    elif kind == "w_wide":
                        wh, part = divmod(step[1], 2)
                        w, half = divmod(wh, 2)
                        n = open_work(plan, step)
                        pe.wait_ge(w_wide_cast, w + 1)
                        for i in range(MT // 2):
                            m = part * (MT // 2) + i
                            at = m * D + half * P if w < 2 else half * HID + m * P
                            ins = pe.transpose(bank32(n)[:, i * P:(i + 1) * P], w32[:, at:at + P], ident32[:, :])
                        ins.then_inc(work_filled, 1)
                    elif kind == "q_wide":
                        _, b, g = step
                        n = open_work(plan, step)
                        pe.wait_ge(normed1, plan.nth[of("norm1"), 2 * b + 1] + 1)
                        for qt in range(QT):
                            slot = ln_slot(plan, step[0], 1, 2 * b + qt // 2)
                            ins = pe.transpose(bank32(n)[:, qt * P:(qt + 1) * P],
                                               norm32[:, slot, qt % 2, g * P:(g + 1) * P], ident32[:, :])
                        ins.then_inc(work_filled, 1)
                    elif kind == "k_block":
                        _, b, c, g = step
                        n = open_work(plan, step)
                        pe.wait_ge(kv_rest_loaded, 16 * (b + 1))
                        pe.wait_ge(kv_loaded[b], 16)
                        pe.transpose(bank32(n)[:, 0:P], chunk_kv(b, c)[:, g * P:(g + 1) * P], ident32[:, :]
                                     ).then_inc(work_filled, 1)
                    elif kind == "row_max":
                        _, b, c, qt, g = step
                        n = open_work(plan, step)
                        pe.wait_ge(*plan.emptied((of("mask_rows"), b) if is_wide else ("mask_rows",)))
                        if is_wide:
                            pe.wait_ge(*plan.emptied((of("q_wide"), b, g)))
                            pe.wait_ge(*plan.emptied((of("k_block"), b, c, g)))
                            pe.matmul(bank32(n), q_wide[:, g, qt * P:(qt + 1) * P],
                                      k_blocks[:, c, g * HG:(g + 1) * HG, :], start=True, stop=False,
                                      skip_group_check=True)
                        else:
                            pe.wait_ge(*plan.emptied(("q_stack", b, qt)))
                            pe.wait_ge(*plan.emptied(("k_stack", b)))
                            for j in range(HG):
                                h = g * HG + j
                                pe.matmul(bank32(n)[:, j * P:(j + 1) * P], q_stacks[:, b, h, qt * P:(qt + 1) * P],
                                          k_stacks[:, b, h, :], start=(j == 0), stop=False, skip_group_check=True)
                        rows = bias_rows[:, b * NC + c, :].unsqueeze(1).to_broadcast((P, HG, P))
                        pe.matmul(bank32(n), ones_b[:, :], rows, start=False, stop=True, skip_group_check=True
                                  ).then_inc(work_filled, 1)
                    elif kind == "max_t":
                        n = open_work(plan, step)
                        pe.wait_ge(max_split, plan.nth[step] + 1)
                        for t in range(2):
                            ins = pe.transpose(bankb(n)[:, t * P:(t + 1) * P],
                                               max_cols[:, 2 * (step[1] % 2) + t, :], identb[:, :])
                        ins.then_inc(work_filled, 1)
                    elif kind == "scores":
                        _, b, half, g, c, pair = step
                        j = plan.nth[step]
                        if j == 0:
                            pe.wait_ge(selector_ready, 1)
                        if j >= 2:
                            pe.wait_ge(exp_done, j - 1)
                        pe.wait_ge(*plan.emptied((of("max_t"), 2 * b + half)))
                        rows = plan.nth[of("max_t"), 2 * b + half] % 2
                        at = slice(half * SH, (half + 1) * SH)
                        for i in range(2):
                            h = g * HG + 2 * pair + i
                            dst = bank32(SCORES[j % 2])[:, i * SH:(i + 1) * SH]
                            if is_wide:
                                pe.matmul(dst, k_blocks[:, c, h, :], q_wide[:, g, at], start=(i == 0), stop=False,
                                          skip_group_check=True)
                            else:
                                pe.matmul(dst, k_stacks[:, b, h, :], q_stacks[:, b, h, at], start=(i == 0),
                                          stop=False, skip_group_check=True)
                            ins = pe.matmul(dst, max_sel[:, h, :], max_rows[:, rows, :], start=False, stop=True,
                                            skip_group_check=True)
                        ins.then_inc(scores_filled, 1)
                    elif kind in ("weigh_o", "weigh_d"):
                        _, b, half, g, c = step
                        values = kind == "weigh_o"
                        first, last = not is_wide or c == 0, c == LAST
                        j0 = plan.nth[of("scores"), b, half, g, c, 0]
                        pe.wait_ge(exp_done, j0 + 2)
                        if is_wide and (b, half, g, c) == (0, 0, 0, 0) and not values:
                            for read in plan.early_users(HID_BANKS[0]):
                                pe.wait_ge(*read)
                        if first or not values:
                            before = plan.nth[of("o_copy"), b, half, g]
                            if values and before:
                                pe.wait_ge(o_copied, before)
                            if not values and before > g:
                                pe.wait_ge(o_copied, before - g)
                        for j in range(HG):
                            h = g * HG + j
                            part = slice(j * DH, (j + 1) * DH)
                            pr = probs[:, (j0 + j // 2) % NPB, (j % 2) * SH:(j % 2 + 1) * SH]
                            if values:
                                ins = pe.matmul(bank32(O_BANK)[part, 0:SH],
                                                chunk_kv(b, c)[:, D + h * DH:D + (h + 1) * DH], pr,
                                                start=first, stop=last, tile_position=(0, j * DH),
                                                skip_group_check=True)
                            else:
                                ins = pe.matmul(sums_at(is_wide)[part, :], sum_cols[:, g, :], pr,
                                                start=(is_wide and g == 0 and c == 0), stop=(last and g == NG - 1),
                                                tile_position=(0, j * DH), skip_group_check=True)
                        if not values:
                            ins.then_inc(weighed, 1)
                        elif last:
                            ins.then_inc(o_summed, 1)
                    elif kind == "attn_t":
                        _, b, qt = step
                        n = open_work(plan, step)
                        copied = plan.nth[of("o_copy"), b, qt // 2, NG - 1]
                        pe.wait_ge(o_copied, copied + 1)
                        at = slice((qt % 2) * P, (qt % 2 + 1) * P)
                        for g in range(NG + 1):
                            ins = pe.transpose(bank32(n)[:, g * P:(g + 1) * P],
                                               o_sb[:, (copied // NG) % 2, g, at], ident32[:, :])
                        ins.then_inc(work_filled, 1)
                    elif kind == "n_t":
                        r = step[1]
                        n = open_work(plan, step)
                        if is_wide:
                            pe.wait_ge(normed2, plan.nth[of("norm2"), r] + 1)
                        else:
                            pe.wait_ge(norm_high, plan.nth["high", 2, r] + 1)
                            pe.wait_ge(norm_low, plan.nth["low", 2, r] + 1)
                        for lk in range(KD if is_wide else 2 * KD):
                            for t in range(2):
                                at = slice((2 * lk + t) * P, (2 * lk + t + 1) * P)
                                l, k = divmod(lk, KD)
                                cols = slice(k * P, (k + 1) * P)
                                if is_wide:
                                    slot = ln_slot(plan, step[0], 2, r)
                                    ins = pe.transpose(bank32(n)[:, at], norm32[:, slot, t, cols], ident32[:, :])
                                else:
                                    ins = pe.transpose(bank16(n)[:, at], norm16[:, r % 2, l, t, cols],
                                                       ident16[:, :])
                        ins.then_inc(work_filled, 1)
                    elif kind == "hidden":
                        _, r, m = step
                        n = r * MT + m
                        if m == 0:
                            pe.wait_ge(*plan.emptied((of("n_t"), r)))
                            if r == 0:
                                for i in range(12 if is_wide else 6):
                                    pe.wait_ge(*plan.emptied((of("w_wide" if is_wide else "w_t"), i)))
                                if is_wide:
                                    pe.wait_ge(o_copied, len(plan.of_kind["o_copy"]))
                        if n >= 2:
                            pe.wait_ge(h_made, n - 1)
                        else:
                            for read in plan.early_users(HID_BANKS[n]):
                                pe.wait_ge(*read)
                        for w in range(2):
                            dst = bank32(HID_BANKS[n % 2])[:, w * SH:(w + 1) * SH]
                            terms = [(k, l) for k in range(KD) for l in range(1 if is_wide else 2)]
                            for k, l in terms:
                                at = slice(m * P, (m + 1) * P)
                                if is_wide:
                                    lhs, rhs = w_gu_t32[:, w, k, at], n_t32[:, r % 2, k, :]
                                else:
                                    lhs, rhs = w_gu_t[:, w, k, at], n_t16[:, r % 2, l * KD + k, :]
                                ins = pe.matmul(dst, lhs, rhs, start=(w == 0 and (k, l) == terms[0]),
                                                stop=(k, l) == terms[-1], skip_group_check=True)
                        ins.then_inc(hid_filled, 1)
                    elif kind == "down":
                        _, r, m = step
                        n = r * MT + m
                        if is_wide:
                            pe.wait_ge(h_made, n + 1)
                        else:
                            pe.wait_ge(h_high, n + 1)
                            pe.wait_ge(h_low, n + 1)
                        if m == 0 and r >= 1:
                            pe.wait_ge(y_read, r)
                        for t in range(2):
                            dst = bank32(Y_BANK)[:, t * D:(t + 1) * D]
                            rows = slice(t * P, (t + 1) * P)
                            for l in range(1 if is_wide else 2):
                                if is_wide:
                                    lhs, rhs = h_wide[:, r % 2, m, rows], w_d_t32[:, m, :]
                                else:
                                    lhs, rhs = h16[:, r % 2, m, l, rows], w_d_t[:, m, :]
                                ins = pe.matmul(dst, lhs, rhs, start=(m == 0 and t == 0 and l == 0),
                                                stop=(m == MT - 1), skip_group_check=True)
                        ins.then_inc(down_done, 1)

            run(plans[False], common)
            pe.wait_ge(flag_ready, 1)
            flag = pe.value_load(wide_flag[0:1, 0:1], min_val=0, max_val=2)
            with pe.If(flag > 0):
                run(plans[True], branch[True])
            with pe.Else():
                run(plans[False], narrow)


_INS = ['x', 'ctx_2048', 'mask_BxS2_ik0', 'g_xattn', 'g_ffn', 'L0_xattn_b', 'L0_ffn_w_gate', 'L0_ffn_w_up',
        'L0_ffn_w_down']
_OUTS = [((4, 512, 256), 'float32')]


def kernel(**inputs):
    import numpy as _np
    import concourse.bacc as _bacc
    from concourse import mybir as _mybir
    from concourse.bass_utils import run_bass_kernel_spmd as _run

    nc = _bacc.Bacc("TRN2", target_bir_lowering=False, num_devices=1)
    arrays, args = {}, []
    for name in _INS:
        a = _np.ascontiguousarray(inputs[name])
        arrays[f"in_{name}_dram"] = a
        args.append(nc.dram_tensor(f"in_{name}_dram", a.shape, _mybir.dt.from_np(a.dtype), kind="ExternalInput").ap())
    for i, (shape, dtype) in enumerate(_OUTS):
        dt = _mybir.dt.from_np(_np.dtype(dtype))
        args.append(nc.dram_tensor(f"out_{i}_dram", shape, dt, kind="ExternalOutput").ap())
    flamingo_block_kernel(nc, *args)
    r = _run(nc, [arrays], core_ids=[0])
    got = tuple(r.results[0][f"out_{i}_dram"] for i in range(len(_OUTS)))
    return got[0]
```
